# Optimizing a Trainium2 kernel written in Bass

```python
import numpy as np
import jax
import jax.numpy as jnp

def _softmax(x, axis=-1):
    return jax.nn.softmax(x, axis=axis)

def _gelu(x):
    return jax.nn.gelu(x, approximate=True)

def _silu(x):
    return jax.nn.silu(x)

def _sigmoid(x):
    return jax.nn.sigmoid(x)

def _layernorm(x, axis=-1, eps=1e-05):
    m = jnp.mean(x, axis=axis, keepdims=True)
    v = jnp.var(x, axis=axis, keepdims=True)
    return (x - m) / jnp.sqrt(v + eps)

def _scatter_add(tgt, idx, src, axis=0):
    return tgt.at[idx].add(src)

def _segment_sum(src, seg, n):
    return jax.ops.segment_sum(src, seg, n)
kernel_name = 'mk_gnn_resnorm_d2_gnn_r32_e09616'

def setup_inputs(seed: int=0):
    np.random.seed(seed)
    _w = jnp.asarray

    def _rec_inputs():
        import jax
        import jax.numpy as jnp
        _gk = jax.random.key(seed)
        x = -0.000364 + 1 * jax.random.normal(jax.random.fold_in(_gk, 1), (10000, 768), jnp.float32)
        _s = jax.random.randint(jax.random.fold_in(_gk, 2), (5000,), 0, 10000, jnp.int32)
        _d = jax.random.randint(jax.random.fold_in(_gk, 3), (5000,), 0, 10000, jnp.int32)
        _loop = jnp.arange(10000, dtype=jnp.int32)
        src = jnp.concatenate([_s, _d, _loop])
        dst = jnp.concatenate([_d, _s, _loop])
        _o = jnp.argsort(dst, stable=True)
        src = src[_o]
        dst = dst[_o]
        return (x, src, dst)
    x, src, dst = _rec_inputs()

    def _L0_gnn_setup():
        import jax, jax.numpy as jnp
        import numpy as np
        N_NODES = 625
        N_EDGES = 3125
        D_IN = 768
        NEG_SLOPE = 0.2

        def _gat_layer(x, W, attn_l, attn_r, bias, src, dst, num_heads, head_dim, use_elu):
            N = x.shape[0]
            z = (x @ W).reshape(N, num_heads, head_dim)
            el = jnp.sum(z * attn_l, axis=-1)
            er = jnp.sum(z * attn_r, axis=-1)
            e = jax.nn.leaky_relu(el[src] + er[dst], NEG_SLOPE)
            m = jax.ops.segment_max(e, dst, num_segments=N)
            ex = jnp.exp(e - m[dst])
            denom = jax.ops.segment_sum(ex, dst, num_segments=N)
            alpha = ex / denom[dst]
            msg = alpha[:, :, None] * z[src]
            out = jax.ops.segment_sum(msg, dst, num_segments=N)
            out = out + z
            out = out + bias.reshape(1, num_heads, head_dim)
            if use_elu:
                out = jax.nn.elu(out)
            return out.reshape(N, num_heads * head_dim)
        key = jax.random.key(seed)
        ks = jax.random.split(key, 16)
        node_features = jax.random.normal(ks[0], (N_NODES, D_IN), dtype=jnp.float32)
        src = jax.random.randint(ks[1], (N_EDGES,), 0, N_NODES)
        dst = jax.random.randint(ks[2], (N_EDGES,), 0, N_NODES)
        s = 1.0 / np.sqrt(D_IN)
        inp = {'node_features': node_features, 'src': src, 'dst': dst}
        heads = [(12, 64), (12, 64), (1, 768)]
        for i, (H, D) in enumerate(heads):
            inp[f'W{i}'] = jax.random.normal(ks[3 + 4 * i], (D_IN, H * D), dtype=jnp.float32) * s
            inp[f'al{i}'] = jax.random.normal(ks[4 + 4 * i], (H, D), dtype=jnp.float32) * s
            inp[f'ar{i}'] = jax.random.normal(ks[5 + 4 * i], (H, D), dtype=jnp.float32) * s
            inp[f'b{i}'] = jnp.zeros((H * D,), dtype=jnp.float32)
        return inp
    _L0_gnn_all = _L0_gnn_setup()
    _L0_gnn_in = {k: v for k, v in _L0_gnn_all.items() if k in ('W0', 'al0', 'ar0', 'b0', 'W1', 'al1', 'ar1', 'b1', 'W2', 'al2', 'ar2', 'b2')}
    del _L0_gnn_all

    def _L1_gnn_setup():
        import jax, jax.numpy as jnp
        import numpy as np
        N_NODES = 10000
        NEG_SLOPE = 0.2
        EPS = 1e-16

        def gat_layer(x, W, att_src, att_dst, bias, src, dst, heads, out_ch, concat):
            n = x.shape[0]
            h = (x @ W.T).reshape(n, heads, out_ch)
            a_src = jnp.einsum('nhc,hc->nh', h, att_src)
            a_dst = jnp.einsum('nhc,hc->nh', h, att_dst)
            e = a_src[src] + a_dst[dst]
            e = jax.nn.leaky_relu(e, NEG_SLOPE)
            m = jax.ops.segment_max(e, dst, num_segments=n)
            ex = jnp.exp(e - m[dst])
            denom = jax.ops.segment_sum(ex, dst, num_segments=n)
            alpha = ex / (denom[dst] + EPS)
            msg = alpha[:, :, None] * h[src]
            out = jax.ops.segment_sum(msg, dst, num_segments=n)
            if concat:
                out = out.reshape(n, heads * out_ch)
            else:
                out = out.mean(axis=1)
            return out + bias
        key = jax.random.key(seed)
        ks = jax.random.split(key, 12)
        x = jax.random.normal(ks[0], (N_NODES, 768), dtype=jnp.float32)
        edge_index = jax.random.randint(ks[1], (2, 5000), 0, N_NODES, dtype=jnp.int64)
        s1 = 1.0 / np.sqrt(768.0)
        W1 = jax.random.normal(ks[2], (8 * 128, 768), dtype=jnp.float32) * s1
        att_src1 = jax.random.normal(ks[3], (8, 128), dtype=jnp.float32) * (1.0 / np.sqrt(128.0))
        att_dst1 = jax.random.normal(ks[4], (8, 128), dtype=jnp.float32) * (1.0 / np.sqrt(128.0))
        b1 = jnp.zeros((8 * 128,), dtype=jnp.float32)
        s2 = 1.0 / np.sqrt(1024.0)
        W2 = jax.random.normal(ks[5], (1 * 768, 1024), dtype=jnp.float32) * s2
        att_src2 = jax.random.normal(ks[6], (1, 768), dtype=jnp.float32) * (1.0 / np.sqrt(768.0))
        att_dst2 = jax.random.normal(ks[7], (1, 768), dtype=jnp.float32) * (1.0 / np.sqrt(768.0))
        b2 = jnp.zeros((768,), dtype=jnp.float32)
        return {'x': x, 'edge_index': edge_index, 'W1': W1, 'att_src1': att_src1, 'att_dst1': att_dst1, 'b1': b1, 'W2': W2, 'att_src2': att_src2, 'att_dst2': att_dst2, 'b2': b2}
    _L1_gnn_all = _L1_gnn_setup()
    _L1_gnn_in = {k: v for k, v in _L1_gnn_all.items() if k in ('W1', 'att_src1', 'att_dst1', 'b1', 'W2', 'att_src2', 'att_dst2', 'b2')}
    del _L1_gnn_all
    return {'x': x, 'src': src, 'dst': dst, 'L0_gnn_W0': _L0_gnn_in['W0'], 'L0_gnn_al0': _L0_gnn_in['al0'], 'L0_gnn_ar0': _L0_gnn_in['ar0'], 'L0_gnn_b0': _L0_gnn_in['b0'], 'L0_gnn_W1': _L0_gnn_in['W1'], 'L0_gnn_al1': _L0_gnn_in['al1'], 'L0_gnn_ar1': _L0_gnn_in['ar1'], 'L0_gnn_b1': _L0_gnn_in['b1'], 'L0_gnn_W2': _L0_gnn_in['W2'], 'L0_gnn_al2': _L0_gnn_in['al2'], 'L0_gnn_ar2': _L0_gnn_in['ar2'], 'L0_gnn_b2': _L0_gnn_in['b2'], 'L1_gnn_W1': _L1_gnn_in['W1'], 'L1_gnn_att_src1': _L1_gnn_in['att_src1'], 'L1_gnn_att_dst1': _L1_gnn_in['att_dst1'], 'L1_gnn_b1': _L1_gnn_in['b1'], 'L1_gnn_W2': _L1_gnn_in['W2'], 'L1_gnn_att_src2': _L1_gnn_in['att_src2'], 'L1_gnn_att_dst2': _L1_gnn_in['att_dst2'], 'L1_gnn_b2': _L1_gnn_in['b2']}

def reference(x, src, dst, L0_gnn_W0, L0_gnn_al0, L0_gnn_ar0, L0_gnn_b0, L0_gnn_W1, L0_gnn_al1, L0_gnn_ar1, L0_gnn_b1, L0_gnn_W2, L0_gnn_al2, L0_gnn_ar2, L0_gnn_b2, L1_gnn_W1, L1_gnn_att_src1, L1_gnn_att_dst1, L1_gnn_b1, L1_gnn_W2, L1_gnn_att_src2, L1_gnn_att_dst2, L1_gnn_b2):
    import jax
    import jax.numpy as jnp

    def _L0_gnn_ref(node_features, W0, al0, ar0, b0, W1, al1, ar1, b1, W2, al2, ar2, b2, src, dst):
        import jax, jax.numpy as jnp
        import numpy as np
        N_NODES = 625
        N_EDGES = 3125
        D_IN = 768
        NEG_SLOPE = 0.2

        def _gat_layer(x, W, attn_l, attn_r, bias, src, dst, num_heads, head_dim, use_elu):
            N = x.shape[0]
            z = (x @ W).reshape(N, num_heads, head_dim)
            el = jnp.sum(z * attn_l, axis=-1)
            er = jnp.sum(z * attn_r, axis=-1)
            e = jax.nn.leaky_relu(el[src] + er[dst], NEG_SLOPE)
            m = jax.ops.segment_max(e, dst, num_segments=N)
            ex = jnp.exp(e - m[dst])
            denom = jax.ops.segment_sum(ex, dst, num_segments=N)
            alpha = ex / denom[dst]
            msg = alpha[:, :, None] * z[src]
            out = jax.ops.segment_sum(msg, dst, num_segments=N)
            out = out + z
            out = out + bias.reshape(1, num_heads, head_dim)
            if use_elu:
                out = jax.nn.elu(out)
            return out.reshape(N, num_heads * head_dim)
        x = _gat_layer(node_features, W0, al0, ar0, b0, src, dst, 12, 64, True)
        x = _gat_layer(x, W1, al1, ar1, b1, src, dst, 12, 64, True)
        x = _gat_layer(x, W2, al2, ar2, b2, src, dst, 1, 768, False)
        return x

    def _L1_gnn_ref(x, edge_index, W1, att_src1, att_dst1, b1, W2, att_src2, att_dst2, b2):
        import jax, jax.numpy as jnp
        import numpy as np
        N_NODES = 10000
        NEG_SLOPE = 0.2
        EPS = 1e-16

        def gat_layer(x, W, att_src, att_dst, bias, src, dst, heads, out_ch, concat):
            n = x.shape[0]
            h = (x @ W.T).reshape(n, heads, out_ch)
            a_src = jnp.einsum('nhc,hc->nh', h, att_src)
            a_dst = jnp.einsum('nhc,hc->nh', h, att_dst)
            e = a_src[src] + a_dst[dst]
            e = jax.nn.leaky_relu(e, NEG_SLOPE)
            m = jax.ops.segment_max(e, dst, num_segments=n)
            ex = jnp.exp(e - m[dst])
            denom = jax.ops.segment_sum(ex, dst, num_segments=n)
            alpha = ex / (denom[dst] + EPS)
            msg = alpha[:, :, None] * h[src]
            out = jax.ops.segment_sum(msg, dst, num_segments=n)
            if concat:
                out = out.reshape(n, heads * out_ch)
            else:
                out = out.mean(axis=1)
            return out + bias
        src, dst = (edge_index[0], edge_index[1])
        h = gat_layer(x, W1, att_src1, att_dst1, b1, src, dst, heads=8, out_ch=128, concat=True)
        h = jax.nn.relu(h)
        out = gat_layer(h, W2, att_src2, att_dst2, b2, src, dst, heads=1, out_ch=768, concat=True)
        return out
    edge_index = jnp.stack([src, dst])
    x = _layernorm(x + _L0_gnn_ref(x, L0_gnn_W0, L0_gnn_al0, L0_gnn_ar0, L0_gnn_b0, L0_gnn_W1, L0_gnn_al1, L0_gnn_ar1, L0_gnn_b1, L0_gnn_W2, L0_gnn_al2, L0_gnn_ar2, L0_gnn_b2, src, dst), axis=-1)
    x = _layernorm(x + _L1_gnn_ref(x, edge_index, L1_gnn_W1, L1_gnn_att_src1, L1_gnn_att_dst1, L1_gnn_b1, L1_gnn_W2, L1_gnn_att_src2, L1_gnn_att_dst2, L1_gnn_b2), axis=-1)
    return x

_drawn_inputs = setup_inputs


def setup_inputs(seed=0):
    import zlib

    import numpy as np

    out = dict(_drawn_inputs(seed))
    spreads = {'L0_gnn_b0': (0.0, 0.1),
     'L0_gnn_b1': (0.0, 0.1),
     'L0_gnn_b2': (0.0, 0.1),
     'L1_gnn_b1': (0.0, 0.1),
     'L1_gnn_b2': (0.0, 0.1)}
    factors = {'L0_gnn_ar0': 12.373,
     'L0_gnn_ar1': 32.37,
     'L0_gnn_ar2': 2.793,
     'L1_gnn_att_dst1': 13.46,
     'L1_gnn_att_src2': 6.198,
     'L1_gnn_att_dst2': 22.989}
    for name, (base, spread) in spreads.items():
        noise = np.random.default_rng([zlib.crc32(name.encode()), seed]).standard_normal(out[name].shape)
        drawn = base * np.exp(spread * noise) if base else spread * noise
        out[name] = jnp.asarray(drawn.astype(out[name].dtype))
    for name, factor in factors.items():
        out[name] = (out[name] * factor).astype(out[name].dtype)
    return out
```

```python
from contextlib import ExitStack

import concourse.bass as bass
from concourse import mybir

ALU = mybir.AluOpType
ACT = mybir.ActivationFunctionType
F32 = mybir.dt.float32
I32 = mybir.dt.int32
AX = mybir.AxisListType.X

P = 128
NODES = 10000
TILES = (NODES + P - 1) // P
ROWS = TILES * P
EDGES = 20000
EC = (EDGES + P - 1) // P
EPAD = EC * P
D = 768
DW = 1024
SLOPE = 0.2
LN_EPS = 1e-5
FAR = 1 << 20
NONE = -2e30
FLOOR = -1e30
BUCKETS = 8
RING = 4
START, LEN, SELF, NODE, SRC = 0, 1, 2, 3, 4
ROW = 8
STEPS, FURTHER = TILES, 2 * TILES + 1
ZMAX = 1044


class Layer:

    def __init__(self, din, heads, dim, eps, residual):
        self.din, self.heads, self.dim = din, heads, dim
        self.out = heads * dim
        self.kc = din // P
        self.groups = 2 if self.out == D else 3
        self.width = -(-(self.out + 2 * heads) // (2 * self.groups)) * 2 * self.groups
        self.cols = self.width // self.groups
        self.eps, self.residual = eps, residual


LAYERS = [Layer(D, 12, 64, 1e-30, True), Layer(D, 12, 64, 1e-30, True), Layer(D, 1, 768, 1e-30, True),
          Layer(D, 8, 128, 1e-16, False), Layer(DW, 1, 768, 1e-16, False)]
AFTER = ["elu", "elu", "norm_x", "relu", "norm_y"]


class Tile:

    def __init__(self, t, par, use):
        self.t, self.par, self.use = t, par, use

    def back(self, n):
        if (self.par + n) % 2 == self.par:
            return Tile(self.t - n, self.par, self.use - n // 2)
        if self.par == 1:
            return Tile(self.t - n, 0, self.use - (n - 1) // 2)
        return Tile(self.t - n, 1, self.use - (n + 1) // 2)


def tile_loop(eng, body, peel):
    for t in range(peel):
        body(Tile(t, t % 2, t // 2))
    with eng.Fori(0, (TILES - peel) // 2) as i:
        body(Tile(i * 2 + peel, 1, i + peel // 2))
        body(Tile(i * 2 + peel + 1, 0, i + peel // 2 + 1))


LAST = Tile(TILES - 1, (TILES - 1) % 2, (TILES - 1) // 2)
USES = [(TILES + 1) // 2, TILES // 2]


def gat_program(nc, x_tiles, x_rows, dst_ext, src_ext, edge_no, node_rows, ident_in, before_in,
                weights, lefts, rights, biases, out):
    with ExitStack() as ctx:
        def sb(name, shape, dt=F32):
            return ctx.enter_context(nc.sbuf_tensor(name, shape, dt))

        def sem(name):
            return ctx.enter_context(nc.semaphore(name))

        z_dram = [nc.dram_tensor(f"z{a}_rows", (ROWS, L.width), F32).ap() for a, L in enumerate(LAYERS)]
        y_dram = nc.dram_tensor("y_rows", (ROWS, D), F32).ap()
        node_tab = nc.dram_tensor("node_tab", (ROWS, ROW), I32).ap()
        place_tab = nc.dram_tensor("place_tab", (ROWS, ROW), I32).ap()

        w_sb = [sb(f"w{a}", [P, L.kc, L.width]) for a, L in enumerate(LAYERS)]
        own_nb = sb("own_nb", [P, 2, 2, ZMAX])
        extra = sb("extra", [P, 2, ZMAX])
        acc = sb("acc", [P, DW])
        prod = sb("prod", [P, DW])
        expo = sb("expo", [P, DW])
        h = sb("h", [P, 2, DW])
        hT = sb("hT", [P, 2, DW])
        zout = sb("zout", [P, 2, ZMAX])
        bias = sb("bias", [P, 2, DW])
        resid = sb("resid", [P, 2, D])
        normed = sb("normed", [P, 2, D])
        ident = sb("ident", [P, P])
        before = sb("before", [P, P])
        ones = sb("ones", [P, P])

        dst_i = sb("dst_i", [P, 3, EC], I32)
        src_i = sb("src_i", [P, 3, EC], I32)
        edge_i = sb("edge_i", [P, EC], I32)
        scans = sb("scans", [P, 5, EC])
        erow = sb("erow", [P, EC, ROW + 1], I32)
        lasts = sb("lasts", [P, 5])
        carried = sb("carried", [P, 4, P + 1])
        carry = sb("carry", [P, 4])
        counts = sb("counts", [P, 6, BUCKETS])
        rank_f = sb("rank_f", [P, TILES])
        rank_i = sb("rank_i", [P, 2, TILES], I32)
        stage = sb("stage", [P, RING, ROW + 1], I32)
        idx_tab = sb("idx_tab", [P, TILES, 4], I32)
        mask_tab = sb("mask_tab", [P, TILES, 2])
        len_tab = sb("len_tab", [P, TILES, 2])
        sched = sb("sched", [P, 3 * TILES + 3], I32)
        slots = sb("slots", [P, 4])
        gidx = sb("gidx", [P, 2, 4], I32)
        sidx = sb("sidx", [P, 2, 1], I32)
        yidx = sb("yidx", [P, 2, 1], I32)
        gslot = sb("gslot", [P, 2])
        gfar = sb("gfar", [P, 2])
        gedge_f = sb("gedge_f", [P, 2])
        gedge = sb("gedge", [P, 2], I32)
        gsrc = sb("gsrc", [P, 2], I32)
        glen = sb("glen", [P, 2])
        e_s = sb("e_s", [P, 2, 12])
        m_s = sb("m_s", [P, 2, 12])
        dif = sb("dif", [P, 3, 12])
        p_s = sb("p_s", [P, 3, 12])
        den = sb("den", [P, 2, 12])
        rden = sb("rden", [P, 12])
        w_s = sb("w_s", [P, 3, 12])
        xslot = sb("xslot", [P, 2])
        xmask = sb("xmask", [P, 2])
        stats = sb("stats", [P, 2, 6])
        mean_var = sb("mean_var", [P, 2])
        rstd = sb("rstd", [P, 2])

        leftright = [own_nb[:, 0], own_nb[:, 1], extra, h, resid]
        onehot = normed[:, 0, 0:BUCKETS * TILES]
        running = normed[:, 1, 0:BUCKETS * TILES]
        zeros = acc[:, 0:EC]
        across = acc[:, 2 * P:7 * P]
        most = scans[:, 0:2, :].rearrange("p q c -> p (q c)")
        erow_flat = erow[:].rearrange("p c k -> p (c k)")
        nload = erow_flat[:, 0:TILES * ROW].rearrange("p (c k) -> p c k", k=ROW)
        nrow = erow_flat[:, TILES * ROW:TILES * (2 * ROW + 1)].rearrange("p (c k) -> p c k", k=ROW + 1)
        one_row = expo[:, 0:BUCKETS * TILES]
        keep = expo[:, BUCKETS * TILES:BUCKETS * TILES + EC]
        etmp = prod[:, D:D + EC]

        zps = ctx.enter_context(nc.psum_tensor("zps", [P, 2, 3, 512], F32))
        tps = ctx.enter_context(nc.psum_tensor("tps", [P, 1024], F32))

        edges_in = sem("edges_in")
        consts_in = sem("consts_in")
        rows_in = sem("rows_in")
        w_in = [sem(f"w_in{a}") for a in range(5)]
        x_in = [sem(f"x_in{i}") for i in range(2)]
        z0_out = [sem(f"z0_out{i}") for i in range(2)]
        bias_in = [sem(f"bias_in{i}") for i in range(2)]
        wchain = sem("wchain")
        chain = sem("chain")
        xchain = sem("xchain")
        gcopied = sem("gcopied")
        scopied = sem("scopied")
        ycopied = sem("ycopied")
        gchain = sem("gchain")
        achain = sem("achain")
        w_ready = sem("w_ready")
        lasts_ready = sem("lasts_ready")
        lasts_turned = sem("lasts_turned")
        carry_ready = sem("carry_ready")
        carry_turned = sem("carry_turned")
        staged = sem("staged")
        ring_out = [sem(f"ring_out{i}") for i in range(RING)]
        nodes_in = sem("nodes_in")
        places_in = sem("places_in")
        counted = sem("counted")
        counts_summed = sem("counts_summed")
        lens_ready = sem("lens_ready")
        lens_turned = sem("lens_turned")
        most_ready = sem("most_ready")
        most_turned = sem("most_turned")
        tables_ready = sem("tables_ready")
        waits_met = sem("waits_met")
        cleared = sem("cleared")
        gathered = [sem(f"gathered{i}") for i in range(2)]
        rows_used = sem("rows_used")
        dif_ready = sem("dif_ready")
        exp_ready = sem("exp_ready")
        xdif_ready = sem("xdif_ready")
        xexp_ready = sem("xexp_ready")
        extra_in = sem("extra_in")
        extra_used = sem("extra_used")
        src_in = sem("src_in")
        acc_ready = sem("acc_ready")
        elu_ready = sem("elu_ready")
        rstd_ready = sem("rstd_ready")
        h_ready = sem("h_ready")
        normed_ready = sem("normed_ready")
        turned = sem("turned")
        hT_ready = sem("hT_ready")
        mm_done = sem("mm_done")
        z_ready = sem("z_ready")
        z_out = [sem(f"z_out{i}") for i in range(2)]
        y_out = [sem(f"y_out{i}") for i in range(2)]

        block = ctx.enter_context(nc.Block())

        def alone(eng):
            eng.sem_inc(waits_met, 1)

        def heads_of(ap, L):
            return ap.rearrange("p (h d) -> p h d", h=L.heads)

        def over_dim(ap, L):
            return ap.unsqueeze(2).to_broadcast([P, L.heads, L.dim])

        @block.sync
        def _(sp):
            for k in range(3):
                sp.dma_start(dst_i[:, k, :], dst_ext[k:k + EPAD].rearrange("(p c) -> p c", c=EC)).then_inc(edges_in, 16)
                sp.dma_start(src_i[:, k, :], src_ext[k:k + EPAD].rearrange("(p c) -> p c", c=EC)).then_inc(edges_in, 16)
            sp.dma_start(edge_i[:], edge_no).then_inc(edges_in, 16)
            sp.dma_start(ident[:], ident_in).then_inc(consts_in, 16)
            sp.dma_start(before[:], before_in).then_inc(consts_in, 16)
            sp.dma_start(node_tab, node_rows).then_inc(rows_in, 16)

            def load_weights(a):
                L = LAYERS[a]
                sp.dma_start(w_sb[a][:, :, 0:L.out], weights[a].rearrange("(c p) n -> p c n", p=P)).then_inc(w_in[a], 16)
                sp.dma_start(leftright[a][:, 0, 0:L.out], lefts[a].to_broadcast([P, L.out])).then_inc(w_in[a], 16)
                sp.dma_start(leftright[a][:, 1, 0:L.out], rights[a].to_broadcast([P, L.out])).then_inc(w_in[a], 16)

            def load_bias(a):
                L = LAYERS[a]
                sp.dma_start(bias[:, a % 2, 0:L.out], biases[a].to_broadcast([P, L.out])).then_inc(bias_in[a % 2], 16)

            load_weights(0)
            for a in range(1, 5):
                load_weights(a)
            load_bias(0)
            load_bias(1)

            def store_z0(T):
                sp.wait_ge(z_ready, T.t + 1)
                sp.dma_start(z_dram[0].rearrange("(t p) n -> t p n", p=P)[bass.ds(T.t, 1)].rearrange("t p n -> (t p) n"),
                             zout[:, T.par, 0:LAYERS[0].width]).then_inc(z0_out[T.par], 16)

            def move(T):
                if not (isinstance(T.t, int) and T.t < 2):
                    sp.wait_ge(mm_done, T.t - 1)
                sp.dma_start(hT[:, T.par, 0:D], x_tiles[bass.ds(T.t, 1)].rearrange("t p n -> (t p) n")).then_inc(x_in[T.par], 16)
                if not (isinstance(T.t, int) and T.t < 2):
                    store_z0(T.back(2))

            tile_loop(sp, move, 3)
            store_z0(LAST.back(1))
            store_z0(LAST)
            for a in range(2, 5):
                sp.wait_ge(rows_used, TILES * (a - 1))
                load_bias(a)

        @block.tensor
        def _(pe):
            def products(a, T):
                L = LAYERS[a]
                for g in range(L.groups):
                    for c in range(L.kc):
                        mm = pe.matmul(zps[:, T.par, g, 0:L.cols], hT[:, T.par, c * P:(c + 1) * P],
                                       w_sb[a][:, c, g * L.cols:(g + 1) * L.cols],
                                       start=(c == 0), stop=(c == L.kc - 1))
                mm.then_inc(mm_done, 1)

            def first_layer(T):
                pe.wait_ge(x_in[T.par], (T.use + 1) * 16)
                if not (isinstance(T.t, int) and T.t < 2):
                    pe.wait_ge(z_ready, T.t - 1)
                products(0, T)

            pe.wait_ge(consts_in, 32)
            pe.wait_ge(lasts_ready, 1)
            for q in range(5):
                turn = pe.transpose(tps[0:1, q * P:(q + 1) * P], lasts[:, q:q + 1], ident[:])
            turn.then_inc(lasts_turned, 1)
            pe.wait_ge(carry_ready, 1)
            for q in range(4):
                turn = pe.transpose(tps[:, 640 + q:641 + q], carried[0:1, q, 0:P], ident[0:1, 0:1])
            turn.then_inc(carry_turned, 1)
            pe.wait_ge(w_ready, 1)
            part = 43
            first_layer(Tile(0, 0, 0))
            first_layer(Tile(1, 1, 0))
            first_layer(Tile(2, 0, 1))
            with pe.Fori(1, part // 2) as i:
                first_layer(Tile(i * 2 + 1, 1, i))
                first_layer(Tile(i * 2 + 2, 0, i + 1))
            pe.wait_ge(counted, 1)
            pe.matmul(tps[:, 0:BUCKETS], before[:], counts[:, 0, :], start=True, stop=True)
            pe.matmul(tps[:, 512:512 + BUCKETS], ones[:], counts[:, 0, :], start=True, stop=True).then_inc(counts_summed, 1)
            with pe.Fori(part // 2, TILES // 2) as i:
                first_layer(Tile(i * 2 + 1, 1, i))
                first_layer(Tile(i * 2 + 2, 0, i + 1))
            pe.wait_ge(lens_ready, 1)
            pe.transpose(tps[0:TILES, 0:P], len_tab[:, :, 0], ident[:]).then_inc(lens_turned, 1)
            pe.wait_ge(most_ready, 1)
            pe.transpose(tps[0:1, 512:512 + TILES], most[0:TILES, 0:1], ident[0:TILES, 0:TILES]).then_inc(most_turned, 1)
            pe.wait_ge(tables_ready, 1)

            for a in range(1, 5):
                L = LAYERS[a]
                base = (a - 1) * TILES

                def turn_h(T):
                    pe.wait_ge(h_ready, T.t + base + 1)
                    if not (isinstance(T.t, int) and T.t + base == 0):
                        pe.wait_ge(hT_ready, T.t + base)
                    for c in range(L.kc):
                        src = normed if AFTER[a - 1] == "norm_x" else h
                        turn = pe.transpose(tps[:, c * P:(c + 1) * P], src[:, T.par, c * P:(c + 1) * P], ident[:])
                    turn.then_inc(turned, 1)

                def multiply(T):
                    pe.wait_ge(hT_ready, T.t + base + 1)
                    pe.wait_ge(z_ready, T.t + a * TILES - 1)
                    products(a, T)

                def step(T):
                    turn_h(T)
                    if not isinstance(T.t, int):
                        multiply(T.back(1))

                tile_loop(pe, step, 1)
                multiply(LAST)

        @block.scalar
        def _(act):
            def take_z(a, T):
                L = LAYERS[a]
                act.wait_ge(mm_done, T.t + a * TILES + 1)
                act.activation(zout[:, T.par, 0:L.width].rearrange("p (g n) -> p g n", g=L.groups),
                               zps[:, T.par, 0:L.groups, 0:L.cols], ACT.Copy).then_inc(z_ready, 1)

            def first_layer(T):
                if not (isinstance(T.t, int) and T.t < 2):
                    act.wait_ge(z0_out[T.par], T.use * 16)
                take_z(0, T)

            tile_loop(act, first_layer, 3)
            act.wait_ge(tables_ready, 1)
            for a in range(5):
                L = LAYERS[a]
                base = a * TILES
                total = act.value_load(sched[0:1, STEPS + TILES:STEPS + TILES + 1], min_val=0, max_val=EDGES)
                step_base = total * a

                def weigh(T):
                    act.wait_ge(dif_ready, T.t + base + 1)
                    act.activation(p_s[:, 0:2, 0:L.heads], dif[:, 0:2, 0:L.heads], ACT.Exp).then_inc(exp_ready, 1)
                    n = act.value_load(sched[0:1, bass.ds(T.t, 1)], min_val=0, max_val=EDGES)
                    done = act.value_load(sched[0:1, bass.ds(T.t + STEPS, 1)], min_val=0, max_val=EDGES)
                    with act.If(n > 0):
                        with act.Fori(0, n) as j:
                            act.wait_ge(xdif_ready, step_base + done + j + 1)
                            act.activation(p_s[:, :, 0:L.heads], dif[:, :, 0:L.heads], ACT.Exp).then_inc(xexp_ready, 1)

                def finish(T):
                    if AFTER[a] == "elu":
                        elus = (a * TILES + T.t)
                        act.wait_ge(acc_ready, elus + 1)
                        act.activation(prod[:, 0:D], acc[:, 0:D], ACT.Relu, scale=-1.0).then_inc(achain, 1)
                        act.wait_ge(achain, elus + 1)
                        act.activation(expo[:, 0:D], prod[:, 0:D], ACT.Exp, scale=-1.0).then_inc(elu_ready, 1)
                    if AFTER[a].startswith("norm"):
                        norms = (TILES * (1 if a == 4 else 0)) + T.t
                        act.wait_ge(acc_ready, 2 * TILES + norms + 1)
                        act.activation(rstd[:, 0:1], mean_var[:, 1:2], ACT.Ln).then_inc(achain, 1)
                        act.wait_ge(achain, 2 * TILES + norms + 1)
                        act.activation(rstd[:, 1:2], rstd[:, 0:1], ACT.Exp, scale=-0.5).then_inc(rstd_ready, 1)

                def take_h(T):
                    M = LAYERS[a + 1]
                    act.wait_ge(turned, T.t + base + 1)
                    act.wait_ge(mm_done, T.t + (a + 1) * TILES - 1)
                    if AFTER[a] == "relu":
                        act.activation(hT[:, T.par, 0:M.din], tps[:, 0:M.din], ACT.Relu).then_inc(hT_ready, 1)
                    else:
                        act.activation(hT[:, T.par, 0:M.din], tps[:, 0:M.din], ACT.Copy,
                                       bias=-1.0 if AFTER[a] == "elu" else 0.0).then_inc(hT_ready, 1)

                def free_and_take_z(T, first_two):
                    if not first_two:
                        act.wait_ge(z_out[T.par], (USES[T.par] * a + T.use) * 16)
                    take_z(a + 1, T)

                def step(T):
                    weigh(T)
                    finish(T)
                    if a < 4:
                        take_h(T)
                        if not (isinstance(T.t, int) and T.t == 0):
                            free_and_take_z(T.back(1), isinstance(T.t, int) and T.t <= 2)

                tile_loop(act, step, 3)
                if a < 4:
                    free_and_take_z(LAST, False)

        @block.gpsimd
        def _(pool):
            def scatter(ncols, before_cols, table):
                def column(c, j):
                    pool.wait_ge(staged, c + before_cols + 1)
                    alone(pool)
                    pool.indirect_dma_start(
                        out=table, out_offset=bass.IndirectOffsetOnAxis(ap=stage[:, j, ROW:ROW + 1], axis=0),
                        in_=stage[:, j, 0:ROW], in_offset=None, bounds_check=ROWS - 1, oob_is_err=False,
                    ).then_inc(ring_out[j], 16)
                with pool.Fori(0, ncols // RING) as r:
                    for j in range(RING):
                        column(r * RING + j, j)
                for j in range(ncols % RING):
                    column(ncols // RING * RING + j, j)

            pool.wait_ge(rows_in, 16)
            scatter(EC, 0, node_tab)
            for j in range(RING):
                pool.wait_ge(ring_out[j], 16 * ring_uses(EC, j))
            pool.dma_start(nload[:], node_tab.rearrange("(p c) k -> p c k", p=P)).then_inc(nodes_in, 16)
            scatter(TILES, EC, place_tab)
            for j in range(RING):
                pool.wait_ge(ring_out[j], 16 * (ring_uses(EC, j) + ring_uses(TILES, j)))
            pool.dma_start(nload[:], place_tab.rearrange("(p c) k -> p c k", p=P)).then_inc(places_in, 16)
            pool.wait_ge(tables_ready, 1)

            def rows_of(table, target, index, signal):
                pool.indirect_dma_start(
                    out=target, out_offset=None, in_=table,
                    in_offset=bass.IndirectOffsetOnAxis(ap=index, axis=0),
                    bounds_check=ROWS - 1, oob_is_err=False).then_inc(signal, 16)

            def to_rows(table, source, index, signal):
                pool.indirect_dma_start(
                    out=table, out_offset=bass.IndirectOffsetOnAxis(ap=index, axis=0),
                    in_=source, in_offset=None, bounds_check=ROWS - 1, oob_is_err=False).then_inc(signal, 16)

            for a in range(5):
                L = LAYERS[a]
                norm = AFTER[a].startswith("norm")
                base = a * TILES
                norms = TILES * (1 if a == 4 else 0)
                for i in range(2):
                    if a == 0:
                        pool.wait_ge(z0_out[i], 16 * USES[i])
                    else:
                        pool.wait_ge(z_out[i], 16 * USES[i] * a)
                    if a == 4:
                        pool.wait_ge(y_out[i], 16 * USES[i])
                total = pool.value_load(sched[0:1, STEPS + TILES:STEPS + TILES + 1], min_val=0, max_val=EDGES)
                further = pool.value_load(sched[0:1, FURTHER + TILES:FURTHER + TILES + 1], min_val=0, max_val=EDGES)
                step_base, further_base = total * a, further * a

                def fetch(T):
                    if isinstance(T.t, int) and T.t < 2:
                        if a:
                            pool.wait_ge(rows_used, base)
                    else:
                        pool.wait_ge(rows_used, T.t + base - 1)
                        alone(pool)
                    pool.tensor_copy(gidx[:, T.par, :], idx_tab[:, bass.ds(T.t, 1), :].rearrange("p t k -> p (t k)")).then_inc(gcopied, 1)
                    pool.tensor_copy(glen[:], len_tab[:, bass.ds(T.t, 1), :].rearrange("p t k -> p (t k)")).then_inc(gcopied, 1)
                    pool.tensor_copy(gslot[:], slots[:, 2:4]).then_inc(gcopied, 1)
                    pool.wait_ge(gcopied, (T.t + base + 1) * 3)
                    alone(pool)
                    for k in range(2):
                        rows_of(z_dram[a], own_nb[:, T.par, k, 0:L.width], gidx[:, T.par, k:k + 1], gathered[T.par])
                    if norm:
                        rows_of(x_rows if a == 2 else y_dram, resid[:, T.par, :], gidx[:, T.par, 0:1], gathered[T.par])

                def fetch_extra(T):
                    n = pool.value_load(sched[0:1, bass.ds(T.t, 1)], min_val=0, max_val=EDGES)
                    done = pool.value_load(sched[0:1, bass.ds(T.t + STEPS, 1)], min_val=0, max_val=EDGES)
                    done_further = pool.value_load(sched[0:1, bass.ds(T.t + FURTHER, 1)], min_val=0, max_val=EDGES)
                    with pool.If(n > 0):
                        pool.wait_ge(extra_used, step_base + done + 1)
                        alone(pool)
                        for k in range(2):
                            rows_of(z_dram[a], extra[:, k, 0:L.width], gidx[:, T.par, 2 + k:3 + k], extra_in)
                    with pool.If(n > 1):
                        with pool.Fori(1, n) as j:
                            g = further_base + done_further + j - 1
                            pool.tensor_scalar(gfar[:], gslot[:], glen[:, 0:1], float(FAR), ALU.is_ge, ALU.mult).then_inc(gchain, 1)
                            pool.tensor_scalar(gedge_f[:], gslot[:], glen[:, 1:2], None, ALU.add).then_inc(gchain, 1)
                            pool.memset(gsrc[:], FAR).then_inc(gchain, 1)
                            pool.wait_ge(gchain, g * 6 + 3)
                            alone(pool)
                            pool.tensor_tensor(gedge_f[:], gedge_f[:], gfar[:], ALU.add).then_inc(gchain, 1)
                            pool.tensor_scalar(gslot[:], gslot[:], 2.0, None, ALU.add).then_inc(gchain, 1)
                            pool.wait_ge(gchain, g * 6 + 5)
                            alone(pool)
                            pool.tensor_copy(gedge[:], gedge_f[:]).then_inc(gchain, 1)
                            pool.wait_ge(gchain, g * 6 + 6)
                            alone(pool)
                            for k in range(2):
                                pool.indirect_dma_start(
                                    out=gsrc[:, k:k + 1], out_offset=None, in_=src_ext.rearrange("(n o) -> n o", o=1),
                                    in_offset=bass.IndirectOffsetOnAxis(ap=gedge[:, k:k + 1], axis=0),
                                    bounds_check=EDGES - 1, oob_is_err=False).then_inc(src_in, 16)
                            pool.wait_ge(src_in, g * 32 + 32)
                            alone(pool)
                            pool.wait_ge(extra_used, step_base + done + j + 1)
                            alone(pool)
                            for k in range(2):
                                rows_of(z_dram[a], extra[:, k, 0:L.width], gsrc[:, k:k + 1], extra_in)
                            pool.wait_ge(extra_in, (step_base + done + j) * 32 + 32)
                            alone(pool)

                def spread_z(T):
                    pool.wait_ge(z_ready, T.t + base + TILES + 1)
                    alone(pool)
                    pool.tensor_copy(sidx[:, T.par, :], idx_tab[:, bass.ds(T.t, 1), 0:1].rearrange("p t k -> p (t k)")).then_inc(scopied, 1)
                    pool.wait_ge(scopied, T.t + base + 1)
                    alone(pool)
                    to_rows(z_dram[a + 1], zout[:, T.par, 0:LAYERS[a + 1].width], sidx[:, T.par, :], z_out[T.par])

                def spread_y(T):
                    pool.wait_ge(normed_ready, T.t + norms + 1)
                    alone(pool)
                    pool.tensor_copy(yidx[:, T.par, :], idx_tab[:, bass.ds(T.t, 1), 0:1].rearrange("p t k -> p (t k)")).then_inc(ycopied, 1)
                    pool.wait_ge(ycopied, T.t + norms + 1)
                    alone(pool)
                    to_rows(y_dram if a == 2 else out, normed[:, T.par, :], yidx[:, T.par, :], y_out[T.par])

                def step(T):
                    fetch(T)
                    fetch_extra(T)
                    if norm and not (isinstance(T.t, int) and T.t < 1):
                        spread_y(T.back(1))
                    if a < 4 and not (isinstance(T.t, int) and T.t < 3):
                        spread_z(T.back(3))

                tile_loop(pool, step, 3)
                if norm:
                    spread_y(LAST)
                if a < 4:
                    for n in (2, 1, 0):
                        spread_z(LAST.back(n))
            for i in range(2):
                pool.wait_ge(y_out[i], 16 * 2 * USES[i])

        @block.vector
        def _(dve):
            chained = [0]

            def link(ins):
                ins.then_inc(chain, 1)
                chained[0] += 1
                dve.wait_ge(chain, chained[0])

            link(dve.memset(acc[:], 0.0))
            link(dve.memset(one_row[:], 1.0))
            link(dve.memset(ones[:], 1.0))
            link(dve.memset(carried[:], 0.0))
            for k in range(4):
                link(dve.memset(slots[:, k:k + 1], float(k + 1)))
            for a, L in enumerate(LAYERS):
                used = L.out + 2 * L.heads
                if used < L.width:
                    link(dve.memset(w_sb[a][:, :, used:L.width], 0.0))
            dve.wait_ge(edges_in, 16 * 7)
            prv, dst, nxt = dst_i[:, 0, :], dst_i[:, 1, :], dst_i[:, 2, :]
            link(dve.tensor_tensor(keep[:], dst, prv, ALU.is_equal))
            link(dve.tensor_tensor_scan(scans[:, 0, :], keep[:], zeros, 1.0, ALU.mult, ALU.add))
            for q in range(4):
                said = edge_i[:] if q == 0 else src_i[:, q - 1, :]
                link(dve.tensor_tensor(etmp[:], said, keep[:], ALU.mult))
                link(dve.tensor_tensor(etmp[:], said, etmp[:], ALU.subtract))
                link(dve.tensor_tensor_scan(scans[:, q + 1, :], keep[:], etmp[:], 0.0, ALU.mult, ALU.add))
            dve.tensor_copy(lasts[:], scans[:, :, EC - 1]).then_inc(lasts_ready, 1)
            dve.wait_ge(lasts_turned, 1)
            link(dve.tensor_copy(across[0:1, :], tps[0:1, 0:5 * P]))
            for q in range(4):
                scan = dve.tensor_tensor_scan(carried[0:1, q, 1:P + 1], across[0:1, 0:P],
                                              across[0:1, (q + 1) * P:(q + 2) * P], 0.0, ALU.mult, ALU.add)
                if q < 3:
                    link(scan)
            scan.then_inc(carry_ready, 1)
            dve.wait_ge(carry_ready, 1)
            dve.wait_ge(carry_turned, 1)
            link(dve.tensor_copy(carry[:], tps[:, 640:644]))
            for q in range(4):
                link(dve.scalar_tensor_tensor(scans[:, q + 1, :], scans[:, 0, :], carry[:, q:q + 1],
                                              scans[:, q + 1, :], ALU.mult, ALU.add))
            link(dve.tensor_copy(erow[:, :, START], scans[:, 1, :]))
            link(dve.tensor_copy(erow[:, :, NODE], dst))
            for k in range(3):
                link(dve.tensor_copy(erow[:, :, SRC + k], scans[:, 2 + k, :]))
            link(dve.memset(erow[:, :, ROW - 1:ROW], 0))
            link(dve.tensor_tensor(etmp[:], src_i[:, 0, :], dst, ALU.is_equal))
            link(dve.tensor_copy(erow[:, :, SELF], etmp[:]))
            link(dve.tensor_tensor(etmp[:], edge_i[:], etmp[:], ALU.subtract))
            link(dve.scalar_tensor_tensor(erow[:, :, LEN], etmp[:], 1.0, scans[:, 1, :], ALU.add, ALU.subtract))
            link(dve.tensor_tensor(etmp[:], dst, nxt, ALU.is_equal))
            link(dve.scalar_tensor_tensor(erow[:, :, ROW], etmp[:], float(FAR), dst, ALU.mult, ALU.add))

            wchained = [0]

            def wlink(ins, at):
                ins.then_inc(wchain, 1)
                dve.wait_ge(wchain, at)

            def score_columns(a):
                L = LAYERS[a]
                dve.wait_ge(w_in[a], 48)
                with dve.Fori(0, L.kc) as c:
                    for side in range(2):
                        w = w_sb[a][:, bass.ds(c, 1), :].rearrange("p t n -> p (t n)")
                        at = c * 4 + (wchained[0] + side * 2)
                        wlink(dve.tensor_tensor(prod[:, 0:L.out], w[:, 0:L.out], leftright[a][:, side, 0:L.out], ALU.mult), at + 1)
                        wlink(dve.tensor_reduce(w[:, L.out + side * L.heads:L.out + (side + 1) * L.heads],
                                                heads_of(prod[:, 0:L.out], L), AX, ALU.add), at + 2)
                wchained[0] += 4 * L.kc

            score_columns(0)
            dve.sem_inc(w_ready, 1)

            def stage_rows(source, ncols, before_cols):
                def column(c, j, turn):
                    if not (isinstance(turn, int) and turn == 0):
                        dve.wait_ge(ring_out[j], turn * 16)
                    dve.tensor_copy(stage[:, j, :], source[:, bass.ds(c, 1), :].rearrange("p t k -> p (t k)")).then_inc(staged, 1)
                earlier = [ring_uses(before_cols, j) for j in range(RING)]
                for j in range(RING):
                    column(j, j, earlier[j])
                with dve.Fori(1, ncols // RING) as r:
                    for j in range(RING):
                        column(r * RING + j, j, r + earlier[j])
                for j in range(ncols % RING):
                    column(ncols // RING * RING + j, j, ncols // RING + earlier[j])

            stage_rows(erow, EC, 0)

            dve.wait_ge(nodes_in, 16)
            link(dve.tensor_copy(nrow[:, :, 0:ROW], nload[:]))
            for k in range(BUCKETS):
                link(dve.tensor_scalar(onehot[:, k * TILES:(k + 1) * TILES], nload[:, :, LEN], float(BUCKETS - 1),
                                       float(BUCKETS - 1 - k), ALU.min, ALU.is_equal))
            dve.tensor_reduce(counts[:, 0, :], onehot.rearrange("p (k c) -> p k c", k=BUCKETS), AX, ALU.add).then_inc(counted, 1)
            link(dve.tensor_tensor_scan(running, one_row[:, 0:BUCKETS * TILES], onehot, 0.0, ALU.mult, ALU.add))
            dve.wait_ge(counted, 1)
            dve.wait_ge(counts_summed, 1)
            link(dve.tensor_copy(counts[:, 1, :], tps[:, 0:BUCKETS]))
            link(dve.tensor_copy(counts[:, 2, :], tps[:, 512:512 + BUCKETS]))
            link(dve.tensor_tensor_scan(counts[:, 3, :], one_row[:, 0:BUCKETS], counts[:, 2, :], 0.0, ALU.mult, ALU.add))
            link(dve.tensor_tensor_scan(counts[:, 4, :], one_row[:, 0:BUCKETS], counts[:, 0, :], 0.0, ALU.mult, ALU.add))
            link(dve.tensor_tensor(counts[:, 3, :], counts[:, 3, :], counts[:, 2, :], ALU.subtract))
            link(dve.tensor_tensor(counts[:, 4, :], counts[:, 4, :], counts[:, 0, :], ALU.subtract))
            link(dve.tensor_tensor(counts[:, 3, :], counts[:, 3, :], counts[:, 1, :], ALU.add))
            link(dve.tensor_tensor(counts[:, 5, :], counts[:, 3, :], counts[:, 4, :], ALU.subtract))
            for k in range(BUCKETS):
                s = slice(k * TILES, (k + 1) * TILES)
                link(dve.scalar_tensor_tensor(running[:, s], running[:, s], counts[:, 5, k:k + 1], onehot[:, s],
                                              ALU.add, ALU.mult))
            link(dve.tensor_reduce(rank_f[:], running.rearrange("p (k c) -> p c k", k=BUCKETS), AX, ALU.add))
            link(dve.tensor_scalar(rank_i[:, 0, :], rank_f[:], -1.0, None, ALU.add))
            link(dve.tensor_scalar(rank_i[:, 1, :], rank_i[:, 0, :], 7, None, ALU.logical_shift_right))
            link(dve.tensor_scalar(rank_i[:, 0, :], rank_i[:, 0, :], P - 1, None, ALU.bitwise_and))
            link(dve.scalar_tensor_tensor(nrow[:, :, ROW], rank_i[:, 0, :], float(TILES), rank_i[:, 1, :], ALU.mult, ALU.add))
            stage_rows(nrow, TILES, EC)

            for a in range(1, 5):
                score_columns(a)
            link(dve.memset(own_nb[:], 0.0))
            link(dve.memset(extra[:], 0.0))

            dve.wait_ge(places_in, 16)
            link(dve.tensor_copy(idx_tab[:, :, 0], nload[:, :, NODE]))
            for k in range(3):
                link(dve.tensor_scalar(rank_f[:], nload[:, :, LEN], float(k), float(FAR), ALU.is_le, ALU.mult))
                link(dve.tensor_tensor(idx_tab[:, :, 1 + k], rank_f[:], nload[:, :, SRC + k], ALU.add))
            link(dve.tensor_scalar(mask_tab[:, :, 0], nload[:, :, SELF], 0.0, NONE, ALU.is_equal, ALU.mult))
            link(dve.tensor_scalar(mask_tab[:, :, 1], nload[:, :, LEN], 0.0, NONE, ALU.is_le, ALU.mult))
            link(dve.tensor_copy(len_tab[:, :, 1], nload[:, :, START]))
            dve.tensor_copy(len_tab[:, :, 0], nload[:, :, LEN]).then_inc(lens_ready, 1)
            dve.wait_ge(lens_turned, 1)
            dve.tensor_reduce(most[0:TILES, 0:1], tps[0:TILES, 0:P], AX, ALU.max).then_inc(most_ready, 1)
            dve.wait_ge(most_turned, 1)
            link(dve.memset(sched[:], 0))
            link(dve.memset(most[0:1, :], 0.0))
            link(dve.tensor_copy(sched[0:1, 0:TILES], tps[0:1, 512:512 + TILES]))
            link(dve.tensor_scalar(sched[0:1, 0:TILES], sched[0:1, 0:TILES], 1, None, ALU.logical_shift_right))
            link(dve.tensor_copy(most[0:1, 0:TILES], sched[0:1, 0:TILES]))
            link(dve.tensor_tensor_scan(most[0:1, STEPS + 1:STEPS + 1 + TILES], one_row[0:1, 0:TILES], most[0:1, 0:TILES],
                                        0.0, ALU.mult, ALU.add))
            link(dve.tensor_scalar(most[0:1, 0:TILES], most[0:1, 0:TILES], -1.0, 0.0, ALU.add, ALU.max))
            link(dve.tensor_tensor_scan(most[0:1, FURTHER + 1:FURTHER + 1 + TILES], one_row[0:1, 0:TILES], most[0:1, 0:TILES],
                                        0.0, ALU.mult, ALU.add))
            dve.tensor_copy(sched[0:1, STEPS:FURTHER + 1 + TILES], most[0:1, STEPS:FURTHER + 1 + TILES]).then_inc(tables_ready, 1)
            dve.wait_ge(tables_ready, 1)

            dve.sem_inc(extra_used, 1)
            rows_before = [0, 0]
            links_before = chained[0]
            for a in range(5):
                L = LAYERS[a]
                H = L.heads
                norm = AFTER[a].startswith("norm")
                base = a * TILES
                rows_a = 3 if norm else 2
                total = dve.value_load(sched[0:1, STEPS + TILES:STEPS + TILES + 1], min_val=0, max_val=EDGES)
                step_base = total * a
                per_tile = [0]
                dve.wait_ge(bias_in[a % 2], 16 * (a // 2 + 1))

                def weighted(target, rows, weight, add):
                    if H == 1:
                        if add:
                            return [lambda: dve.scalar_tensor_tensor(target, rows, weight, target, ALU.mult, ALU.add)]
                        return [lambda: dve.tensor_scalar(target, rows, weight, None, ALU.mult)]
                    if not add:
                        return [lambda: dve.tensor_tensor(heads_of(target, L), heads_of(rows, L), over_dim(weight, L), ALU.mult)]
                    return [lambda: dve.tensor_tensor(heads_of(prod[:, 0:L.out], L), heads_of(rows, L), over_dim(weight, L), ALU.mult),
                            lambda: dve.tensor_tensor(target, target, prod[:, 0:L.out], ALU.add)]

                def pair(ap):
                    return ap.unsqueeze(1).to_broadcast([P, 2, H])

                def tile(T):
                    here = [0]
                    start = T.t * per_tile[0] + links_before if not isinstance(T.t, int) else links_before + T.t * per_tile[0]

                    def link(ins):
                        ins.then_inc(chain, 1)
                        here[0] += 1
                        dve.wait_ge(chain, start + here[0])

                    dve.wait_ge(gathered[T.par], (T.use * rows_a + (rows_before[T.par] + rows_a)) * 16)
                    rows = own_nb[:, T.par]
                    e, dif2, p2 = e_s[:, :, 0:H], dif[:, 0:2, 0:H], p_s[:, 0:2, 0:H]
                    er = rows[:, 0, L.out + H:L.out + 2 * H]
                    link(dve.tensor_tensor(e, rows[:, :, L.out:L.out + H], pair(er), ALU.add))
                    link(dve.scalar_tensor_tensor(e, e, SLOPE, e, ALU.mult, ALU.max))
                    link(dve.tensor_tensor(e, e, mask_tab[:, bass.ds(T.t, 1), :].rearrange("p t k -> p (t k)").unsqueeze(2).to_broadcast([P, 2, H]), ALU.add))
                    link(dve.scalar_tensor_tensor(m_s[:, 0, 0:H], e_s[:, 0, 0:H], FLOOR, e_s[:, 1, 0:H], ALU.max, ALU.max))
                    dve.tensor_tensor(dif2, e, pair(m_s[:, 0, 0:H]), ALU.subtract).then_inc(dif_ready, 1)
                    link(dve.tensor_copy(xslot[:], slots[:, 0:2]))
                    dve.wait_ge(exp_ready, T.t + base + 1)
                    link(dve.scalar_tensor_tensor(den[:, 0, 0:H], p_s[:, 0, 0:H], L.eps, p_s[:, 1, 0:H], ALU.add, ALU.add))
                    link(dve.reciprocal(rden[:, 0:H], den[:, 0, 0:H]))
                    link(dve.tensor_tensor(w_s[:, 0:2, 0:H], p2, pair(rden[:, 0:H]), ALU.mult))
                    total_ = acc[:, 0:L.out]
                    for k in range(2):
                        for make in weighted(total_, rows[:, k, 0:L.out], w_s[:, k, 0:H], k > 0):
                            link(make())

                    n = dve.value_load(sched[0:1, bass.ds(T.t, 1)], min_val=0, max_val=EDGES)
                    done = dve.value_load(sched[0:1, bass.ds(T.t + STEPS, 1)], min_val=0, max_val=EDGES)
                    with dve.If(n > 0):
                        with dve.Fori(0, n) as j:
                            extra_step(T, er, done, j)

                    v = total_
                    if L.residual:
                        link(dve.tensor_tensor(v, v, rows[:, 0, 0:L.out], ALU.add))
                    if norm:
                        link(dve.tensor_tensor(v, v, resid[:, T.par, :], ALU.add))
                    if AFTER[a] == "relu":
                        dve.wait_ge(turned, T.t + base - 1)
                        dve.tensor_tensor(h[:, T.par, 0:L.out], v, bias[:, a % 2, 0:L.out], ALU.add).then_inc(h_ready, 1)
                        dve.wait_ge(h_ready, T.t + base + 1)
                    else:
                        link(dve.tensor_tensor(v, v, bias[:, a % 2, 0:L.out], ALU.add))
                    dve.sem_inc(rows_used, 1)
                    if AFTER[a] == "elu":
                        dve.sem_inc(acc_ready, 1)
                        dve.wait_ge(elu_ready, T.t + base + 1)
                        if a > 0 or not (isinstance(T.t, int) and T.t < 2):
                            dve.wait_ge(turned, T.t + base - 1)
                        dve.scalar_tensor_tensor(h[:, T.par, 0:D], v, 0.0, expo[:, 0:D], ALU.max, ALU.add).then_inc(h_ready, 1)
                        dve.wait_ge(h_ready, T.t + base + 1)
                    if norm:
                        norms = T.t + TILES * (1 if a == 4 else 0)
                        for g in range(2):
                            link(dve.bn_stats(stats[:, g, :], v[:, g * (D // 2):(g + 1) * (D // 2)]))
                        alone(dve)
                        link(dve.bn_aggr(mean_var[:], stats[:].rearrange("p g s -> p (g s)")))
                        dve.tensor_scalar(mean_var[:, 1:2], mean_var[:, 1:2], LN_EPS, None, ALU.add).then_inc(acc_ready, 1)
                        dve.wait_ge(rstd_ready, norms + 1)
                        if a == 2:
                            dve.wait_ge(turned, T.t + base - 1)
                            if not (isinstance(T.t, int) and T.t < 2):
                                dve.wait_ge(y_out[T.par], T.use * 16)
                        else:
                            dve.wait_ge(y_out[T.par], (T.use + USES[T.par]) * 16)
                        dve.tensor_scalar(normed[:, T.par, :], v, mean_var[:, 0:1], rstd[:, 1:2], ALU.subtract, ALU.mult).then_inc(normed_ready, 1)
                        dve.wait_ge(normed_ready, norms + 1)
                        if a == 2:
                            dve.sem_inc(h_ready, 1)
                    per_tile[0] = here[0]

                X_LINKS = [20, 20, 18, 20, 18]

                def extra_step(T, er, done, j):
                    here = [0]
                    start = total * sum(X_LINKS[:a]) + (done + j) * X_LINKS[a]

                    def link(ins):
                        ins.then_inc(xchain, 1)
                        here[0] += 1
                        dve.wait_ge(xchain, start + here[0])

                    dve.wait_ge(extra_in, (step_base + done + j) * 32 + 32)
                    e = e_s[:, :, 0:H]
                    m0, m1 = m_s[:, 0, 0:H], m_s[:, 1, 0:H]
                    link(dve.tensor_scalar(xmask[:], xslot[:], len_tab[:, bass.ds(T.t, 1), 0:1].rearrange("p t k -> p (t k)"), NONE, ALU.is_ge, ALU.mult))
                    link(dve.tensor_scalar(xslot[:], xslot[:], 2.0, None, ALU.add))
                    link(dve.tensor_tensor(e, extra[:, :, L.out:L.out + H], pair(er), ALU.add))
                    link(dve.scalar_tensor_tensor(e, e, SLOPE, e, ALU.mult, ALU.max))
                    link(dve.tensor_tensor(e, e, xmask[:].unsqueeze(2).to_broadcast([P, 2, H]), ALU.add))
                    link(dve.tensor_tensor(m1, e_s[:, 0, 0:H], m0, ALU.max))
                    link(dve.tensor_tensor(m1, e_s[:, 1, 0:H], m1, ALU.max))
                    link(dve.tensor_tensor(dif[:, 0:2, 0:H], e, pair(m1), ALU.subtract))
                    dve.tensor_tensor(dif[:, 2, 0:H], m0, m1, ALU.subtract).then_inc(xdif_ready, 1)
                    dve.wait_ge(xexp_ready, step_base + done + j + 1)
                    link(dve.tensor_copy(m0, m1))
                    link(dve.tensor_tensor(den[:, 1, 0:H], den[:, 0, 0:H], p_s[:, 2, 0:H], ALU.mult))
                    link(dve.tensor_tensor(rden[:, 0:H], p_s[:, 0, 0:H], p_s[:, 1, 0:H], ALU.add))
                    link(dve.tensor_tensor(den[:, 0, 0:H], den[:, 1, 0:H], rden[:, 0:H], ALU.add))
                    link(dve.reciprocal(rden[:, 0:H], den[:, 0, 0:H]))
                    link(dve.tensor_tensor(w_s[:, 2, 0:H], den[:, 1, 0:H], rden[:, 0:H], ALU.mult))
                    link(dve.tensor_tensor(w_s[:, 0:2, 0:H], p_s[:, 0:2, 0:H], pair(rden[:, 0:H]), ALU.mult))
                    total_ = acc[:, 0:L.out]
                    for make in weighted(total_, total_, w_s[:, 2, 0:H], False):
                        link(make())
                    for k in range(2):
                        for make in weighted(total_, extra[:, k, 0:L.out], w_s[:, k, 0:H], True):
                            link(make())
                    dve.sem_inc(extra_used, 1)
                    assert here[0] == X_LINKS[a], here

                tile_loop(dve, tile, 3)
                links_before += TILES * per_tile[0]
                for i in range(2):
                    rows_before[i] += rows_a * USES[i]


def ring_uses(cols, j):
    return cols // RING + (1 if j < cols % RING else 0)


_WEIGHTS = ["L0_gnn_W0", "L0_gnn_W1", "L0_gnn_W2", "L1_gnn_W1", "L1_gnn_W2"]
_LEFTS = ["L0_gnn_al0", "L0_gnn_al1", "L0_gnn_al2", "L1_gnn_att_src1", "L1_gnn_att_src2"]
_RIGHTS = ["L0_gnn_ar0", "L0_gnn_ar1", "L0_gnn_ar2", "L1_gnn_att_dst1", "L1_gnn_att_dst2"]
_BIASES = ["L0_gnn_b0", "L0_gnn_b1", "L0_gnn_b2", "L1_gnn_b1", "L1_gnn_b2"]


def kernel(**inputs):
    import numpy as np
    import concourse.bacc as bacc
    from concourse.bass_utils import run_bass_kernel_spmd

    arrays, aps = {}, {}
    nc = bacc.Bacc("TRN2", target_bir_lowering=False, num_devices=1)

    def give(name, a):
        a = np.ascontiguousarray(a)
        arrays["in_" + name] = a
        aps[name] = nc.dram_tensor("in_" + name, a.shape, mybir.dt.from_np(a.dtype), kind="ExternalInput").ap()

    x = np.asarray(inputs["x"])
    x_rows = np.concatenate([x, np.zeros((ROWS - NODES, D), x.dtype)])
    give("x_rows", x_rows)
    give("x_tiles", x_rows.reshape(TILES, P, D // P, P).transpose(0, 3, 2, 1).reshape(TILES, P, D))
    dst, src = np.asarray(inputs["dst"]), np.asarray(inputs["src"])
    far = np.full(EPAD - EDGES + 1, FAR, dst.dtype)
    give("dst_ext", np.concatenate([np.full(1, -1, dst.dtype), dst, far]))
    give("src_ext", np.concatenate([src, np.zeros(EPAD - EDGES + 2, src.dtype)]))
    give("edge_no", np.arange(EPAD, dtype=np.int32).reshape(P, EC))
    node_rows = np.zeros((ROWS, ROW), np.int32)
    node_rows[:, NODE] = np.arange(ROWS)
    give("node_rows", node_rows)
    give("ident", np.eye(P, dtype=np.float32))
    give("before", np.triu(np.ones((P, P), np.float32), 1))
    for name in _WEIGHTS:
        w = np.asarray(inputs[name])
        give(name, w.T if name.startswith("L1") else w)
    for name in _LEFTS + _RIGHTS + _BIASES:
        give(name, np.asarray(inputs[name]).reshape(1, -1))
    out = nc.dram_tensor("out_rows", (ROWS, D), F32, kind="ExternalOutput").ap()
    gat_program(nc, aps["x_tiles"], aps["x_rows"], aps["dst_ext"], aps["src_ext"], aps["edge_no"], aps["node_rows"],
                aps["ident"], aps["before"], [aps[n] for n in _WEIGHTS], [aps[n] for n in _LEFTS],
                [aps[n] for n in _RIGHTS], [aps[n] for n in _BIASES], out)
    r = run_bass_kernel_spmd(nc, [arrays], core_ids=[0])
    return r.results[0]["out_rows"][:NODES]
```

```python
from contextlib import ExitStack

import concourse.bass as bass
from concourse import mybir

ALU = mybir.AluOpType
ACT = mybir.ActivationFunctionType
F32 = mybir.dt.float32
I32 = mybir.dt.int32
AX = mybir.AxisListType.X

P = 128
NODES = 10000
TILES = (NODES + P - 1) // P
ROWS = TILES * P
EDGES = 20000
EC = (EDGES + P - 1) // P
EPAD = EC * P
D = 768
DW = 1024
SLOPE = 0.2
LN_EPS = 1e-5
FAR = 1 << 20
NONE = -2e30
FLOOR = -1e30
RSQRT_BITS = 0x5F3759DF
BUCKETS = 8
RING = 4
START, LEN, SELF, NODE, SRC = 0, 1, 2, 3, 4
ROW = 8
STEPS, FURTHER = TILES, 2 * TILES + 1
STEPPED, FURTHERED, LINKED = 3 * TILES + 2, 3 * TILES + 3, 3 * TILES + 4
ZMAX = 1044


class Layer:

    def __init__(self, din, heads, dim, eps, residual):
        self.din, self.heads, self.dim = din, heads, dim
        self.out = heads * dim
        self.kc = din // P
        self.groups = 2 if self.out == D else 3
        self.width = -(-(self.out + 2 * heads) // (2 * self.groups)) * 2 * self.groups
        self.cols = self.width // self.groups
        self.eps, self.residual = eps, residual


LAYERS = [Layer(D, 12, 64, 1e-30, True), Layer(D, 12, 64, 1e-30, True), Layer(D, 1, 768, 1e-30, True),
          Layer(D, 8, 128, 1e-16, False), Layer(DW, 1, 768, 1e-16, False)]
AFTER = ["elu", "elu", "norm_x", "relu", "norm_y"]


class Tile:

    def __init__(self, t, par, use):
        self.t, self.par, self.use = t, par, use

    def ahead(self):
        return Tile(self.t + 1, 1 - self.par, self.use + self.par)

    def back(self, n):
        if n == 0:
            return self
        if (self.par + n) % 2 == self.par:
            return Tile(self.t - n, self.par, self.use - n // 2)
        if self.par == 1:
            return Tile(self.t - n, 0, self.use - (n - 1) // 2)
        return Tile(self.t - n, 1, self.use - (n + 1) // 2)


def tile_loop(eng, body, peel, tail=0):
    for t in range(peel):
        body(Tile(t, t % 2, t // 2))
    pairs = (TILES - peel - tail) // 2
    with eng.Fori(0, pairs) as i:
        for k in range(2):
            par = (peel + k) % 2
            body(Tile(i * 2 + (peel + k), par, i + (peel + k) // 2))
    for t in range(peel + 2 * pairs, TILES):
        body(Tile(t, t % 2, t // 2))


LAST = Tile(TILES - 1, (TILES - 1) % 2, (TILES - 1) // 2)
USES = [(TILES + 1) // 2, TILES // 2]


def gat_program(nc, x_tiles, x_rows, dst_ext, src_ext, edge_no, node_rows, ident_in, before_in,
                weights, lefts, rights, biases, out):
    with ExitStack() as ctx:
        def sb(name, shape, dt=F32):
            return ctx.enter_context(nc.sbuf_tensor(name, shape, dt))

        def sem(name):
            return ctx.enter_context(nc.semaphore(name))

        z_dram = [nc.dram_tensor(f"z{a}_rows", (ROWS, L.width), F32).ap() for a, L in enumerate(LAYERS)]
        y_dram = nc.dram_tensor("y_rows", (ROWS, D), F32).ap()
        node_tab = nc.dram_tensor("node_tab", (ROWS, ROW), I32).ap()
        place_tab = nc.dram_tensor("place_tab", (ROWS, ROW), I32).ap()

        w_sb = [sb(f"w{a}", [P, L.kc, L.width]) for a, L in enumerate(LAYERS)]
        own_nb = sb("own_nb", [P, 2, 2, ZMAX])
        extra = sb("extra", [P, 2, ZMAX])
        acc = sb("acc", [P, DW])
        prod = sb("prod", [P, 2, DW])
        expo = sb("expo", [P, DW])
        h = sb("h", [P, 2, DW])
        hT = sb("hT", [P, 2, DW])
        zout = sb("zout", [P, 2, ZMAX])
        bias = sb("bias", [P, DW])
        resid = sb("resid", [P, 2, D])
        normed = sb("normed", [P, 2, D])
        ident = sb("ident", [P, P])
        before = sb("before", [P, P])
        ones = sb("ones", [P, P])

        dst_i = sb("dst_i", [P, 3, EC], I32)
        src_i = sb("src_i", [P, 3, EC], I32)
        edge_i = sb("edge_i", [P, EC], I32)
        scans = sb("scans", [P, 5, EC])
        erow = sb("erow", [P, EC, ROW + 1], I32)
        lasts = sb("lasts", [P, 5])
        carried = sb("carried", [P, 4, P + 1])
        carry = sb("carry", [P, 4])
        counts = sb("counts", [P, 6, BUCKETS])
        rank_f = sb("rank_f", [P, TILES])
        rank_i = sb("rank_i", [P, 2, TILES], I32)
        stage = sb("stage", [P, RING, ROW + 1], I32)
        idx_tab = sb("idx_tab", [P, TILES, 4], I32)
        mask_tab = sb("mask_tab", [P, TILES, 2])
        len_tab = sb("len_tab", [P, TILES, 2])
        sched = sb("sched", [P, 3 * TILES + 5], I32)
        slots = sb("slots", [P, 5])
        gidx = sb("gidx", [P, 2, 4], I32)
        sidx = sb("sidx", [P, 2, 1], I32)
        yidx = sb("yidx", [P, 2, 1], I32)
        gslot = sb("gslot", [P, 2])
        gfar = sb("gfar", [P, 2])
        gedge_f = sb("gedge_f", [P, 2])
        gedge = sb("gedge", [P, 2], I32)
        gsrc = sb("gsrc", [P, 2], I32)
        glen = sb("glen", [P, 2])
        relus = expo
        e_s = sb("e_s", [P, 2, 12])
        m_s = sb("m_s", [P, 2, 12])
        dif = sb("dif", [P, 2, 2, 12])
        p_s = sb("p_s", [P, 2, 2, 12])
        den = sb("den", [P, 2, 12])
        rden = sb("rden", [P, 12])
        w_s = sb("w_s", [P, 2, 12])
        xe_s = sb("xe_s", [P, 2, 12])
        xm_s = sb("xm_s", [P, 12])
        xdif = sb("xdif", [P, 3, 12])
        xp_s = sb("xp_s", [P, 3, 12])
        xw_s = sb("xw_s", [P, 4, 12])
        xslot = sb("xslot", [P, 2])
        xmask = sb("xmask", [P, 2])
        stats = sb("stats", [P, 2, 6])
        mean_var = sb("mean_var", [P, 2, 2])
        rstd = sb("rstd", [P, 2, 4], I32)

        leftright = [own_nb[:, 0], own_nb[:, 1], extra, h, resid]
        onehot = normed[:, 0, 0:BUCKETS * TILES]
        running = normed[:, 1, 0:BUCKETS * TILES]
        zeros = acc[:, 0:EC]
        across = acc[:, 2 * P:7 * P]
        most = scans[:, 0:2, :].rearrange("p q c -> p (q c)")
        erow_flat = erow[:].rearrange("p c k -> p (c k)")
        nload = erow_flat[:, 0:TILES * ROW].rearrange("p (c k) -> p c k", k=ROW)
        nrow = erow_flat[:, TILES * ROW:TILES * (2 * ROW + 1)].rearrange("p (c k) -> p c k", k=ROW + 1)
        one_row = expo[:, 0:BUCKETS * TILES]
        keep = expo[:, BUCKETS * TILES:BUCKETS * TILES + EC]
        etmp = prod[:, 1, 0:EC]

        zps = ctx.enter_context(nc.psum_tensor("zps", [P, 2, 3, 512], F32))
        tps = ctx.enter_context(nc.psum_tensor("tps", [P, 1024], F32))

        edges_in = sem("edges_in")
        consts_in = sem("consts_in")
        rows_in = sem("rows_in")
        w_in = [sem(f"w_in{a}") for a in range(5)]
        x_in = [sem(f"x_in{i}") for i in range(2)]
        z0_out = [sem(f"z0_out{i}") for i in range(2)]
        bias_in = sem("bias_in")
        nchain = sem("nchain")
        schain = sem("schain")
        wchain = sem("wchain")
        chain = sem("chain")
        xchain = sem("xchain")
        gcopied = sem("gcopied")
        scopied = sem("scopied")
        ycopied = sem("ycopied")
        gchain = sem("gchain")
        achain = sem("achain")
        w_ready = sem("w_ready")
        lasts_ready = sem("lasts_ready")
        lasts_turned = sem("lasts_turned")
        carry_ready = sem("carry_ready")
        carry_turned = sem("carry_turned")
        staged = sem("staged")
        ring_out = [sem(f"ring_out{i}") for i in range(RING)]
        nodes_in = sem("nodes_in")
        places_in = sem("places_in")
        counted = sem("counted")
        counts_summed = sem("counts_summed")
        lens_ready = sem("lens_ready")
        lens_turned = sem("lens_turned")
        most_ready = sem("most_ready")
        most_turned = sem("most_turned")
        tables_ready = sem("tables_ready")
        waits_met = sem("waits_met")
        cleared = sem("cleared")
        gathered = [sem(f"gathered{i}") for i in range(2)]
        rows_used = sem("rows_used")
        dif_ready = sem("dif_ready")
        exp_ready = sem("exp_ready")
        xdif_ready = sem("xdif_ready")
        xexp_ready = sem("xexp_ready")
        extra_in = sem("extra_in")
        extra_used = sem("extra_used")
        src_in = sem("src_in")
        acc_ready = sem("acc_ready")
        elu_ready = sem("elu_ready")
        rstd_ready = sem("rstd_ready")
        h_ready = sem("h_ready")
        normed_ready = sem("normed_ready")
        turned = sem("turned")
        hT_ready = sem("hT_ready")
        mm_done = sem("mm_done")
        z_ready = sem("z_ready")
        z_out = [sem(f"z_out{i}") for i in range(2)]
        y_out = [sem(f"y_out{i}") for i in range(2)]

        block = ctx.enter_context(nc.Block())

        def alone(eng):
            eng.sem_inc(waits_met, 1)

        def heads_of(ap, L):
            return ap.rearrange("p (h d) -> p h d", h=L.heads)

        def over_dim(ap, L):
            return ap.unsqueeze(2).to_broadcast([P, L.heads, L.dim])

        @block.sync
        def _(sp):
            for k in range(3):
                sp.dma_start(dst_i[:, k, :], dst_ext[k:k + EPAD].rearrange("(p c) -> p c", c=EC)).then_inc(edges_in, 16)
                sp.dma_start(src_i[:, k, :], src_ext[k:k + EPAD].rearrange("(p c) -> p c", c=EC)).then_inc(edges_in, 16)
            sp.dma_start(edge_i[:], edge_no).then_inc(edges_in, 16)
            sp.dma_start(ident[:], ident_in).then_inc(consts_in, 16)
            sp.dma_start(before[:], before_in).then_inc(consts_in, 16)
            sp.dma_start(node_tab, node_rows).then_inc(rows_in, 16)

            def load_weights(a):
                L = LAYERS[a]
                sp.dma_start(w_sb[a][:, :, 0:L.out], weights[a].rearrange("(c p) n -> p c n", p=P)).then_inc(w_in[a], 16)
                sp.dma_start(leftright[a][:, 0, 0:L.out], lefts[a].to_broadcast([P, L.out])).then_inc(w_in[a], 16)
                sp.dma_start(leftright[a][:, 1, 0:L.out], rights[a].to_broadcast([P, L.out])).then_inc(w_in[a], 16)

            def load_bias(a):
                L = LAYERS[a]
                sp.dma_start(bias[:, 0:L.out], biases[a].to_broadcast([P, L.out])).then_inc(bias_in, 16)

            load_weights(0)
            for a in range(1, 5):
                load_weights(a)
            load_bias(0)

            def store_z0(T):
                sp.wait_ge(z_ready, T.t + 1)
                sp.dma_start(z_dram[0].rearrange("(t p) n -> t p n", p=P)[bass.ds(T.t, 1)].rearrange("t p n -> (t p) n"),
                             zout[:, T.par, 0:LAYERS[0].width]).then_inc(z0_out[T.par], 16)

            def move(T):
                if not (isinstance(T.t, int) and T.t < 2):
                    sp.wait_ge(mm_done, T.t - 1)
                sp.dma_start(hT[:, T.par, 0:D], x_tiles[bass.ds(T.t, 1)].rearrange("t p n -> (t p) n")).then_inc(x_in[T.par], 16)
                if not (isinstance(T.t, int) and T.t < 2):
                    store_z0(T.back(2))

            tile_loop(sp, move, 3)
            store_z0(LAST.back(1))
            store_z0(LAST)
            for a in range(1, 5):
                sp.wait_ge(rows_used, TILES * a)
                load_bias(a)

        @block.tensor
        def _(pe):
            def products(a, T):
                L = LAYERS[a]
                for g in range(L.groups):
                    for c in range(L.kc):
                        mm = pe.matmul(zps[:, T.par, g, 0:L.cols], hT[:, T.par, c * P:(c + 1) * P],
                                       w_sb[a][:, c, g * L.cols:(g + 1) * L.cols],
                                       start=(c == 0), stop=(c == L.kc - 1))
                mm.then_inc(mm_done, 1)

            def first_layer(T):
                pe.wait_ge(x_in[T.par], (T.use + 1) * 16)
                if not (isinstance(T.t, int) and T.t < 2):
                    pe.wait_ge(z_ready, T.t - 1)
                products(0, T)

            pe.wait_ge(consts_in, 32)
            pe.wait_ge(lasts_ready, 1)
            for q in range(5):
                turn = pe.transpose(tps[0:1, q * P:(q + 1) * P], lasts[:, q:q + 1], ident[:])
            turn.then_inc(lasts_turned, 1)
            pe.wait_ge(carry_ready, 1)
            for q in range(4):
                turn = pe.transpose(tps[:, 640 + q:641 + q], carried[0:1, q, 0:P], ident[0:1, 0:1])
            turn.then_inc(carry_turned, 1)
            pe.wait_ge(w_ready, 1)
            part = 43
            first_layer(Tile(0, 0, 0))
            first_layer(Tile(1, 1, 0))
            first_layer(Tile(2, 0, 1))
            with pe.Fori(1, part // 2) as i:
                first_layer(Tile(i * 2 + 1, 1, i))
                first_layer(Tile(i * 2 + 2, 0, i + 1))
            pe.wait_ge(counted, 1)
            pe.matmul(tps[:, 0:BUCKETS], before[:], counts[:, 0, :], start=True, stop=True)
            pe.matmul(tps[:, 512:512 + BUCKETS], ones[:], counts[:, 0, :], start=True, stop=True).then_inc(counts_summed, 1)
            with pe.Fori(part // 2, TILES // 2) as i:
                first_layer(Tile(i * 2 + 1, 1, i))
                first_layer(Tile(i * 2 + 2, 0, i + 1))
            pe.wait_ge(lens_ready, 1)
            pe.transpose(tps[0:TILES, 0:P], len_tab[:, :, 0], ident[:]).then_inc(lens_turned, 1)
            pe.wait_ge(most_ready, 1)
            pe.transpose(tps[0:1, 512:512 + TILES], most[0:TILES, 0:1], ident[0:TILES, 0:TILES]).then_inc(most_turned, 1)
            pe.wait_ge(tables_ready, 1)

            for a in range(1, 5):
                L = LAYERS[a]
                base = (a - 1) * TILES

                def turn_h(T):
                    pe.wait_ge(h_ready, T.t + base + 1)
                    if not (isinstance(T.t, int) and T.t + base == 0):
                        pe.wait_ge(hT_ready, T.t + base)
                    for c in range(L.kc):
                        src = normed if AFTER[a - 1] == "norm_x" else h
                        turn = pe.transpose(tps[:, c * P:(c + 1) * P], src[:, T.par, c * P:(c + 1) * P], ident[:])
                    turn.then_inc(turned, 1)

                def multiply(T):
                    pe.wait_ge(hT_ready, T.t + base + 1)
                    pe.wait_ge(z_ready, T.t + a * TILES - 1)
                    products(a, T)

                def step(T):
                    turn_h(T)
                    if not isinstance(T.t, int):
                        multiply(T.back(1))

                tile_loop(pe, step, 1)
                multiply(LAST)

        @block.scalar
        def _(act):
            def take_z(a, T):
                L = LAYERS[a]
                act.wait_ge(mm_done, T.t + a * TILES + 1)
                act.activation(zout[:, T.par, 0:L.width].rearrange("p (g n) -> p g n", g=L.groups),
                               zps[:, T.par, 0:L.groups, 0:L.cols], ACT.Copy).then_inc(z_ready, 1)

            def first_layer(T):
                if not (isinstance(T.t, int) and T.t < 2):
                    act.wait_ge(z0_out[T.par], T.use * 16)
                take_z(0, T)

            tile_loop(act, first_layer, 3)
            act.wait_ge(tables_ready, 1)
            for a in range(5):
                L = LAYERS[a]
                norm = AFTER[a].startswith("norm")
                base = a * TILES
                stepped = act.value_load(sched[0:1, STEPPED:STEPPED + 1], min_val=0, max_val=TILES)
                total = act.value_load(sched[0:1, STEPS + TILES:STEPS + TILES + 1], min_val=0, max_val=EDGES)
                step_base = total * a

                def weigh(T):
                    act.wait_ge(dif_ready, T.t + base + 1)
                    act.activation(p_s[:, T.par, :, 0:L.heads], dif[:, T.par, :, 0:L.heads], ACT.Exp).then_inc(exp_ready, 1)

                def weigh_extra(T):
                    with act.If(stepped > T.t):
                        n = act.value_load(sched[0:1, bass.ds(T.t, 1)], min_val=1, max_val=EDGES)
                        done = act.value_load(sched[0:1, bass.ds(T.t + STEPS, 1)], min_val=0, max_val=EDGES)
                        with act.Fori(0, n) as j:
                            act.wait_ge(xdif_ready, step_base + done + j + 1)
                            act.activation(xp_s[:, :, 0:L.heads], xdif[:, :, 0:L.heads], ACT.Exp).then_inc(xexp_ready, 1)

                def finish(T):
                    if AFTER[a] == "elu":
                        elus = (a * TILES + T.t)
                        act.wait_ge(acc_ready, elus + 1)
                        act.activation(relus[:, 0:D], acc[:, 0:D], ACT.Relu, scale=-1.0).then_inc(achain, 1)
                        act.wait_ge(achain, elus + 1)
                        act.activation(expo[:, 0:D], relus[:, 0:D], ACT.Exp, scale=-1.0).then_inc(elu_ready, 1)
                    if AFTER[a].startswith("norm"):
                        norms = (TILES * (1 if a == 4 else 0)) + T.t
                        act.wait_ge(acc_ready, 2 * TILES + norms + 1)
                        v = mean_var[:, T.par, 1:2]
                        y, y2, vy2, c = (rstd[:, T.par, k:k + 1].bitcast(F32) for k in range(4))
                        at = norms * 11 + 2 * TILES
                        for k in range(3):
                            steps = [lambda: act.activation(y2, y, ACT.Square),
                                     lambda: act.activation(vy2, y2, ACT.Copy, scale=v),
                                     lambda: act.activation(c, vy2, ACT.Identity, scale=-0.5, bias=slots[:, 4:5]),
                                     lambda: act.activation(y, c, ACT.Copy, scale=y)]
                            for m, make in enumerate(steps):
                                if k == 2 and m == 3:
                                    make().then_inc(rstd_ready, 1)
                                else:
                                    make().then_inc(achain, 1)
                                    act.wait_ge(achain, at + (4 * k + m + 1))

                def take_h(T):
                    M = LAYERS[a + 1]
                    act.wait_ge(turned, T.t + base + 1)
                    act.wait_ge(mm_done, T.t + (a + 1) * TILES - 1)
                    if AFTER[a] == "relu":
                        act.activation(hT[:, T.par, 0:M.din], tps[:, 0:M.din], ACT.Relu).then_inc(hT_ready, 1)
                    else:
                        act.activation(hT[:, T.par, 0:M.din], tps[:, 0:M.din], ACT.Copy,
                                       bias=-1.0 if AFTER[a] == "elu" else 0.0).then_inc(hT_ready, 1)

                def free_and_take_z(T, first_two):
                    if not first_two:
                        act.wait_ge(z_out[T.par], (USES[T.par] * a + T.use) * 16)
                    take_z(a + 1, T)

                late = 1 if norm else 0

                def step(T):
                    weigh_extra(T)
                    if not norm:
                        finish(T)
                    if not (isinstance(T.t, int) and T.t == TILES - 1):
                        weigh(T.ahead())
                    if norm:
                        finish(T)
                    if a < 4:
                        if not (isinstance(T.t, int) and T.t < late):
                            take_h(T.back(late))
                        if not (isinstance(T.t, int) and T.t < 2 + late):
                            free_and_take_z(T.back(2 + late), isinstance(T.t, int) and T.t < 4 + late)

                weigh(Tile(0, 0, 0))
                tile_loop(act, step, 5, 1)
                if a < 4:
                    if late:
                        take_h(LAST)
                        free_and_take_z(LAST.back(2), False)
                    free_and_take_z(LAST.back(1), False)
                    free_and_take_z(LAST, False)

        @block.gpsimd
        def _(pool):
            def scatter(ncols, before_cols, table):
                def column(c, j):
                    pool.wait_ge(staged, c + before_cols + 1)
                    alone(pool)
                    pool.indirect_dma_start(
                        out=table, out_offset=bass.IndirectOffsetOnAxis(ap=stage[:, j, ROW:ROW + 1], axis=0),
                        in_=stage[:, j, 0:ROW], in_offset=None, bounds_check=ROWS - 1, oob_is_err=False,
                    ).then_inc(ring_out[j], 16)
                with pool.Fori(0, ncols // RING) as r:
                    for j in range(RING):
                        column(r * RING + j, j)
                for j in range(ncols % RING):
                    column(ncols // RING * RING + j, j)

            pool.wait_ge(rows_in, 16)
            scatter(EC, 0, node_tab)
            for j in range(RING):
                pool.wait_ge(ring_out[j], 16 * ring_uses(EC, j))
            pool.dma_start(nload[:], node_tab.rearrange("(p c) k -> p c k", p=P)).then_inc(nodes_in, 16)
            scatter(TILES, EC, place_tab)
            for j in range(RING):
                pool.wait_ge(ring_out[j], 16 * (ring_uses(EC, j) + ring_uses(TILES, j)))
            pool.dma_start(nload[:], place_tab.rearrange("(p c) k -> p c k", p=P)).then_inc(places_in, 16)
            pool.wait_ge(tables_ready, 1)

            def rows_of(table, target, index, signal):
                pool.indirect_dma_start(
                    out=target, out_offset=None, in_=table,
                    in_offset=bass.IndirectOffsetOnAxis(ap=index, axis=0),
                    bounds_check=ROWS - 1, oob_is_err=False).then_inc(signal, 16)

            def to_rows(table, source, index, signal):
                pool.indirect_dma_start(
                    out=table, out_offset=bass.IndirectOffsetOnAxis(ap=index, axis=0),
                    in_=source, in_offset=None, bounds_check=ROWS - 1, oob_is_err=False).then_inc(signal, 16)

            for a in range(5):
                L = LAYERS[a]
                norm = AFTER[a].startswith("norm")
                base = a * TILES
                norms = TILES * (1 if a == 4 else 0)
                for i in range(2):
                    if a == 0:
                        pool.wait_ge(z0_out[i], 16 * USES[i])
                    else:
                        pool.wait_ge(z_out[i], 16 * USES[i] * a)
                    if a == 4:
                        pool.wait_ge(y_out[i], 16 * USES[i])
                stepped = pool.value_load(sched[0:1, STEPPED:STEPPED + 1], min_val=0, max_val=TILES)
                furthered = pool.value_load(sched[0:1, FURTHERED:FURTHERED + 1], min_val=0, max_val=TILES)
                total = pool.value_load(sched[0:1, STEPS + TILES:STEPS + TILES + 1], min_val=0, max_val=EDGES)
                further = pool.value_load(sched[0:1, FURTHER + TILES:FURTHER + TILES + 1], min_val=0, max_val=EDGES)
                step_base, further_base = total * a, further * a

                def fetch(T):
                    if isinstance(T.t, int) and T.t < 2:
                        if a:
                            pool.wait_ge(rows_used, base)
                    else:
                        pool.wait_ge(rows_used, T.t + base - 1)
                        alone(pool)
                    pool.tensor_copy(gidx[:, T.par, :], idx_tab[:, bass.ds(T.t, 1), :].rearrange("p t k -> p (t k)")).then_inc(gcopied, 1)
                    pool.tensor_copy(glen[:], len_tab[:, bass.ds(T.t, 1), :].rearrange("p t k -> p (t k)")).then_inc(gcopied, 1)
                    pool.tensor_copy(gslot[:], slots[:, 2:4]).then_inc(gcopied, 1)
                    pool.wait_ge(gcopied, (T.t + base + 1) * 3)
                    alone(pool)
                    for k in range(2):
                        rows_of(z_dram[a], own_nb[:, T.par, k, 0:L.width], gidx[:, T.par, k:k + 1], gathered[T.par])
                    if norm:
                        rows_of(x_rows if a == 2 else y_dram, resid[:, T.par, :], gidx[:, T.par, 0:1], gathered[T.par])

                def fetch_extra(T):
                    with pool.If(stepped > T.t):
                        done = pool.value_load(sched[0:1, bass.ds(T.t + STEPS, 1)], min_val=0, max_val=EDGES)
                        pool.wait_ge(extra_used, step_base + done + 1)
                        alone(pool)
                        for k in range(2):
                            rows_of(z_dram[a], extra[:, k, 0:L.width], gidx[:, T.par, 2 + k:3 + k], extra_in)
                    with pool.If(furthered > T.t):
                        n = pool.value_load(sched[0:1, bass.ds(T.t, 1)], min_val=2, max_val=EDGES)
                        done = pool.value_load(sched[0:1, bass.ds(T.t + STEPS, 1)], min_val=0, max_val=EDGES)
                        done_further = pool.value_load(sched[0:1, bass.ds(T.t + FURTHER, 1)], min_val=0, max_val=EDGES)
                        with pool.Fori(1, n) as j:
                            g = further_base + done_further + j - 1
                            pool.tensor_scalar(gfar[:], gslot[:], glen[:, 0:1], float(FAR), ALU.is_ge, ALU.mult).then_inc(gchain, 1)
                            pool.tensor_scalar(gedge_f[:], gslot[:], glen[:, 1:2], None, ALU.add).then_inc(gchain, 1)
                            pool.memset(gsrc[:], FAR).then_inc(gchain, 1)
                            pool.wait_ge(gchain, g * 6 + 3)
                            alone(pool)
                            pool.tensor_tensor(gedge_f[:], gedge_f[:], gfar[:], ALU.add).then_inc(gchain, 1)
                            pool.tensor_scalar(gslot[:], gslot[:], 2.0, None, ALU.add).then_inc(gchain, 1)
                            pool.wait_ge(gchain, g * 6 + 5)
                            alone(pool)
                            pool.tensor_copy(gedge[:], gedge_f[:]).then_inc(gchain, 1)
                            pool.wait_ge(gchain, g * 6 + 6)
                            alone(pool)
                            for k in range(2):
                                pool.indirect_dma_start(
                                    out=gsrc[:, k:k + 1], out_offset=None, in_=src_ext.rearrange("(n o) -> n o", o=1),
                                    in_offset=bass.IndirectOffsetOnAxis(ap=gedge[:, k:k + 1], axis=0),
                                    bounds_check=EDGES - 1, oob_is_err=False).then_inc(src_in, 16)
                            pool.wait_ge(src_in, g * 32 + 32)
                            alone(pool)
                            pool.wait_ge(extra_used, step_base + done + j + 1)
                            alone(pool)
                            for k in range(2):
                                rows_of(z_dram[a], extra[:, k, 0:L.width], gsrc[:, k:k + 1], extra_in)
                            pool.wait_ge(extra_in, (step_base + done + j) * 32 + 32)
                            alone(pool)

                def spread_z(T):
                    pool.wait_ge(z_ready, T.t + base + TILES + 1)
                    alone(pool)
                    pool.tensor_copy(sidx[:, T.par, :], idx_tab[:, bass.ds(T.t, 1), 0:1].rearrange("p t k -> p (t k)")).then_inc(scopied, 1)
                    pool.wait_ge(scopied, T.t + base + 1)
                    alone(pool)
                    to_rows(z_dram[a + 1], zout[:, T.par, 0:LAYERS[a + 1].width], sidx[:, T.par, :], z_out[T.par])

                def spread_y(T):
                    pool.wait_ge(normed_ready, T.t + norms + 1)
                    alone(pool)
                    pool.tensor_copy(yidx[:, T.par, :], idx_tab[:, bass.ds(T.t, 1), 0:1].rearrange("p t k -> p (t k)")).then_inc(ycopied, 1)
                    pool.wait_ge(ycopied, T.t + norms + 1)
                    alone(pool)
                    to_rows(y_dram if a == 2 else out, normed[:, T.par, :], yidx[:, T.par, :], y_out[T.par])

                lag = 5 if norm else 4

                def step(T):
                    fetch(T)
                    fetch_extra(T)
                    if norm and not (isinstance(T.t, int) and T.t < 3):
                        spread_y(T.back(3))
                    if a < 4 and not (isinstance(T.t, int) and T.t < lag):
                        spread_z(T.back(lag))

                tile_loop(pool, step, 5)
                if norm:
                    for n in (2, 1, 0):
                        spread_y(LAST.back(n))
                if a < 4:
                    for n in range(lag - 1, -1, -1):
                        spread_z(LAST.back(n))
            for i in range(2):
                pool.wait_ge(y_out[i], 16 * 2 * USES[i])

        @block.vector
        def _(dve):
            chained = [0]

            def link(ins):
                ins.then_inc(chain, 1)
                chained[0] += 1
                dve.wait_ge(chain, chained[0])

            link(dve.memset(acc[:], 0.0))
            link(dve.memset(one_row[:], 1.0))
            link(dve.memset(ones[:], 1.0))
            link(dve.memset(carried[:], 0.0))
            for k in range(4):
                link(dve.memset(slots[:, k:k + 1], float(k + 1)))
            link(dve.memset(slots[:, 4:5], 1.5))
            for a, L in enumerate(LAYERS):
                used = L.out + 2 * L.heads
                if used < L.width:
                    link(dve.memset(w_sb[a][:, :, used:L.width], 0.0))
            dve.wait_ge(edges_in, 16 * 7)
            prv, dst, nxt = dst_i[:, 0, :], dst_i[:, 1, :], dst_i[:, 2, :]
            link(dve.tensor_tensor(keep[:], dst, prv, ALU.is_equal))
            link(dve.tensor_tensor_scan(scans[:, 0, :], keep[:], zeros, 1.0, ALU.mult, ALU.add))
            for q in range(4):
                said = edge_i[:] if q == 0 else src_i[:, q - 1, :]
                link(dve.tensor_tensor(etmp[:], said, keep[:], ALU.mult))
                link(dve.tensor_tensor(etmp[:], said, etmp[:], ALU.subtract))
                link(dve.tensor_tensor_scan(scans[:, q + 1, :], keep[:], etmp[:], 0.0, ALU.mult, ALU.add))
            dve.tensor_copy(lasts[:], scans[:, :, EC - 1]).then_inc(lasts_ready, 1)
            dve.wait_ge(lasts_turned, 1)
            link(dve.tensor_copy(across[0:1, :], tps[0:1, 0:5 * P]))
            for q in range(4):
                scan = dve.tensor_tensor_scan(carried[0:1, q, 1:P + 1], across[0:1, 0:P],
                                              across[0:1, (q + 1) * P:(q + 2) * P], 0.0, ALU.mult, ALU.add)
                if q < 3:
                    link(scan)
            scan.then_inc(carry_ready, 1)
            dve.wait_ge(carry_ready, 1)
            dve.wait_ge(carry_turned, 1)
            link(dve.tensor_copy(carry[:], tps[:, 640:644]))
            for q in range(4):
                link(dve.scalar_tensor_tensor(scans[:, q + 1, :], scans[:, 0, :], carry[:, q:q + 1],
                                              scans[:, q + 1, :], ALU.mult, ALU.add))
            link(dve.tensor_copy(erow[:, :, START], scans[:, 1, :]))
            link(dve.tensor_copy(erow[:, :, NODE], dst))
            for k in range(3):
                link(dve.tensor_copy(erow[:, :, SRC + k], scans[:, 2 + k, :]))
            link(dve.memset(erow[:, :, ROW - 1:ROW], 0))
            link(dve.tensor_tensor(etmp[:], src_i[:, 0, :], dst, ALU.is_equal))
            link(dve.tensor_copy(erow[:, :, SELF], etmp[:]))
            link(dve.tensor_tensor(etmp[:], edge_i[:], etmp[:], ALU.subtract))
            link(dve.scalar_tensor_tensor(erow[:, :, LEN], etmp[:], 1.0, scans[:, 1, :], ALU.add, ALU.subtract))
            link(dve.tensor_tensor(etmp[:], dst, nxt, ALU.is_equal))
            link(dve.scalar_tensor_tensor(erow[:, :, ROW], etmp[:], float(FAR), dst, ALU.mult, ALU.add))

            wchained = [0]

            def wlink(ins, at):
                ins.then_inc(wchain, 1)
                dve.wait_ge(wchain, at)

            def score_columns(a):
                L = LAYERS[a]
                dve.wait_ge(w_in[a], 48)
                with dve.Fori(0, L.kc) as c:
                    for side in range(2):
                        w = w_sb[a][:, bass.ds(c, 1), :].rearrange("p t n -> p (t n)")
                        at = c * 4 + (wchained[0] + side * 2)
                        wlink(dve.tensor_tensor(prod[:, 0, 0:L.out], w[:, 0:L.out], leftright[a][:, side, 0:L.out], ALU.mult), at + 1)
                        wlink(dve.tensor_reduce(w[:, L.out + side * L.heads:L.out + (side + 1) * L.heads],
                                                heads_of(prod[:, 0, 0:L.out], L), AX, ALU.add), at + 2)
                wchained[0] += 4 * L.kc

            score_columns(0)
            dve.sem_inc(w_ready, 1)

            def stage_rows(source, ncols, before_cols):
                def column(c, j, turn):
                    if not (isinstance(turn, int) and turn == 0):
                        dve.wait_ge(ring_out[j], turn * 16)
                    dve.tensor_copy(stage[:, j, :], source[:, bass.ds(c, 1), :].rearrange("p t k -> p (t k)")).then_inc(staged, 1)
                earlier = [ring_uses(before_cols, j) for j in range(RING)]
                for j in range(RING):
                    column(j, j, earlier[j])
                with dve.Fori(1, ncols // RING) as r:
                    for j in range(RING):
                        column(r * RING + j, j, r + earlier[j])
                for j in range(ncols % RING):
                    column(ncols // RING * RING + j, j, ncols // RING + earlier[j])

            stage_rows(erow, EC, 0)

            dve.wait_ge(nodes_in, 16)
            link(dve.tensor_copy(nrow[:, :, 0:ROW], nload[:]))
            for k in range(BUCKETS):
                link(dve.tensor_scalar(onehot[:, k * TILES:(k + 1) * TILES], nload[:, :, LEN], float(BUCKETS - 1),
                                       float(BUCKETS - 1 - k), ALU.min, ALU.is_equal))
            dve.tensor_reduce(counts[:, 0, :], onehot.rearrange("p (k c) -> p k c", k=BUCKETS), AX, ALU.add).then_inc(counted, 1)
            link(dve.tensor_tensor_scan(running, one_row[:, 0:BUCKETS * TILES], onehot, 0.0, ALU.mult, ALU.add))
            dve.wait_ge(counted, 1)
            dve.wait_ge(counts_summed, 1)
            link(dve.tensor_copy(counts[:, 1, :], tps[:, 0:BUCKETS]))
            link(dve.tensor_copy(counts[:, 2, :], tps[:, 512:512 + BUCKETS]))
            link(dve.tensor_tensor_scan(counts[:, 3, :], one_row[:, 0:BUCKETS], counts[:, 2, :], 0.0, ALU.mult, ALU.add))
            link(dve.tensor_tensor_scan(counts[:, 4, :], one_row[:, 0:BUCKETS], counts[:, 0, :], 0.0, ALU.mult, ALU.add))
            link(dve.tensor_tensor(counts[:, 3, :], counts[:, 3, :], counts[:, 2, :], ALU.subtract))
            link(dve.tensor_tensor(counts[:, 4, :], counts[:, 4, :], counts[:, 0, :], ALU.subtract))
            link(dve.tensor_tensor(counts[:, 3, :], counts[:, 3, :], counts[:, 1, :], ALU.add))
            link(dve.tensor_tensor(counts[:, 5, :], counts[:, 3, :], counts[:, 4, :], ALU.subtract))
            for k in range(BUCKETS):
                s = slice(k * TILES, (k + 1) * TILES)
                link(dve.scalar_tensor_tensor(running[:, s], running[:, s], counts[:, 5, k:k + 1], onehot[:, s],
                                              ALU.add, ALU.mult))
            link(dve.tensor_reduce(rank_f[:], running.rearrange("p (k c) -> p c k", k=BUCKETS), AX, ALU.add))
            link(dve.tensor_scalar(rank_i[:, 0, :], rank_f[:], -1.0, None, ALU.add))
            link(dve.tensor_scalar(rank_i[:, 1, :], rank_i[:, 0, :], 7, None, ALU.logical_shift_right))
            link(dve.tensor_scalar(rank_i[:, 0, :], rank_i[:, 0, :], P - 1, None, ALU.bitwise_and))
            link(dve.scalar_tensor_tensor(nrow[:, :, ROW], rank_i[:, 0, :], float(TILES), rank_i[:, 1, :], ALU.mult, ALU.add))
            stage_rows(nrow, TILES, EC)

            for a in range(1, 5):
                score_columns(a)
            link(dve.memset(own_nb[:], 0.0))
            link(dve.memset(extra[:], 0.0))

            dve.wait_ge(places_in, 16)
            link(dve.tensor_copy(idx_tab[:, :, 0], nload[:, :, NODE]))
            for k in range(3):
                link(dve.tensor_scalar(rank_f[:], nload[:, :, LEN], float(k), float(FAR), ALU.is_le, ALU.mult))
                link(dve.tensor_tensor(idx_tab[:, :, 1 + k], rank_f[:], nload[:, :, SRC + k], ALU.add))
            link(dve.tensor_scalar(mask_tab[:, :, 0], nload[:, :, SELF], 0.0, NONE, ALU.is_equal, ALU.mult))
            link(dve.tensor_scalar(mask_tab[:, :, 1], nload[:, :, LEN], 0.0, NONE, ALU.is_le, ALU.mult))
            link(dve.tensor_copy(len_tab[:, :, 1], nload[:, :, START]))
            dve.tensor_copy(len_tab[:, :, 0], nload[:, :, LEN]).then_inc(lens_ready, 1)
            dve.wait_ge(lens_turned, 1)
            dve.tensor_reduce(most[0:TILES, 0:1], tps[0:TILES, 0:P], AX, ALU.max).then_inc(most_ready, 1)
            dve.wait_ge(most_turned, 1)
            link(dve.memset(sched[:], 0))
            link(dve.memset(most[0:1, :], 0.0))
            link(dve.tensor_copy(sched[0:1, 0:TILES], tps[0:1, 512:512 + TILES]))
            for least, place in ((1, LINKED), (2, STEPPED), (4, FURTHERED)):
                link(dve.tensor_scalar(most[0:1, 0:TILES], tps[0:1, 512:512 + TILES], float(least), None, ALU.is_ge))
                link(dve.tensor_reduce(most[0:1, place:place + 1], most[0:1, 0:TILES], AX, ALU.add))
                link(dve.tensor_copy(sched[0:1, place:place + 1], most[0:1, place:place + 1]))
            link(dve.tensor_scalar(sched[0:1, 0:TILES], sched[0:1, 0:TILES], 1, None, ALU.logical_shift_right))
            link(dve.tensor_copy(most[0:1, 0:TILES], sched[0:1, 0:TILES]))
            link(dve.tensor_tensor_scan(most[0:1, STEPS + 1:STEPS + 1 + TILES], one_row[0:1, 0:TILES], most[0:1, 0:TILES],
                                        0.0, ALU.mult, ALU.add))
            link(dve.tensor_scalar(most[0:1, 0:TILES], most[0:1, 0:TILES], -1.0, 0.0, ALU.add, ALU.max))
            link(dve.tensor_tensor_scan(most[0:1, FURTHER + 1:FURTHER + 1 + TILES], one_row[0:1, 0:TILES], most[0:1, 0:TILES],
                                        0.0, ALU.mult, ALU.add))
            dve.tensor_copy(sched[0:1, STEPS:FURTHER + 1 + TILES], most[0:1, STEPS:FURTHER + 1 + TILES]).then_inc(tables_ready, 1)
            dve.wait_ge(tables_ready, 1)

            dve.sem_inc(extra_used, 1)
            rows_before = [0, 0]
            links_before = chained[0]
            for a in range(5):
                L = LAYERS[a]
                H = L.heads
                norm = AFTER[a].startswith("norm")
                base = a * TILES
                rows_a = 3 if norm else 2
                stepped = dve.value_load(sched[0:1, STEPPED:STEPPED + 1], min_val=0, max_val=TILES)
                linked = dve.value_load(sched[0:1, LINKED:LINKED + 1], min_val=0, max_val=TILES)
                total = dve.value_load(sched[0:1, STEPS + TILES:STEPS + TILES + 1], min_val=0, max_val=EDGES)
                step_base = total * a
                per_tile = [0]
                dve.wait_ge(bias_in, 16 * (a + 1))

                def weighted(target, rows, weight, add):
                    if H == 1:
                        if add:
                            return [lambda: dve.scalar_tensor_tensor(target, rows, weight, target, ALU.mult, ALU.add)]
                        return [lambda: dve.tensor_scalar(target, rows, weight, None, ALU.mult)]
                    if not add:
                        return [lambda: dve.tensor_tensor(heads_of(target, L), heads_of(rows, L), over_dim(weight, L), ALU.mult)]
                    return [lambda: dve.tensor_tensor(heads_of(prod[:, 0, 0:L.out], L), heads_of(rows, L), over_dim(weight, L), ALU.mult),
                            lambda: dve.tensor_tensor(target, target, prod[:, 0, 0:L.out], ALU.add)]

                def pair(ap):
                    return ap.unsqueeze(1).to_broadcast([P, 2, H])

                def total_of(T):
                    return prod[:, T.par, 0:D] if norm else acc[:, 0:L.out]


                def own_er(T):
                    return own_nb[:, T.par, 0, L.out + H:L.out + 2 * H]

                def linker(signal, start, here):
                    def link(ins):
                        ins.then_inc(signal, 1)
                        here[0] += 1
                        dve.wait_ge(signal, start + here[0])
                    return link

                def scores(T):
                    here = [0]
                    link = linker(schain, (T.t + base) * 4, here)
                    dve.wait_ge(gathered[T.par], (T.use * rows_a + (rows_before[T.par] + rows_a)) * 16)
                    rows = own_nb[:, T.par]
                    e = e_s[:, :, 0:H]
                    link(dve.tensor_tensor(e, rows[:, :, L.out:L.out + H], pair(own_er(T)), ALU.add))
                    link(dve.scalar_tensor_tensor(e, e, SLOPE, e, ALU.mult, ALU.max))
                    link(dve.tensor_tensor(e, e, mask_tab[:, bass.ds(T.t, 1), :].rearrange("p t k -> p (t k)").unsqueeze(2).to_broadcast([P, 2, H]), ALU.add))
                    link(dve.scalar_tensor_tensor(m_s[:, T.par, 0:H], e_s[:, 0, 0:H], FLOOR, e_s[:, 1, 0:H], ALU.max, ALU.max))
                    assert here[0] == 4
                    dve.tensor_tensor(dif[:, T.par, :, 0:H], e, pair(m_s[:, T.par, 0:H]), ALU.subtract).then_inc(dif_ready, 1)

                def sums(T, link):
                    total_ = total_of(T)
                    rows = own_nb[:, T.par]
                    link(dve.tensor_copy(xslot[:], slots[:, 0:2]))
                    dve.wait_ge(exp_ready, T.t + base + 1)
                    p2 = p_s[:, T.par, :, 0:H]
                    link(dve.scalar_tensor_tensor(den[:, 0, 0:H], p2[:, 0, :], L.eps, p2[:, 1, :], ALU.add, ALU.add))
                    link(dve.reciprocal(rden[:, 0:H], den[:, 0, 0:H]))
                    link(dve.tensor_tensor(w_s[:, :, 0:H], p2, pair(rden[:, 0:H]), ALU.mult))
                    if L.residual:
                        link(dve.tensor_scalar(w_s[:, 0, 0:H], w_s[:, 0, 0:H], 1.0, None, ALU.add))
                    if H == 1:
                        link(dve.scalar_tensor_tensor(total_, rows[:, 0, 0:L.out], w_s[:, 0, 0:1], bias[:, 0:L.out], ALU.mult, ALU.add))
                        alone(dve)
                        with dve.If(linked > T.t):
                            dve.scalar_tensor_tensor(total_, rows[:, 1, 0:L.out], w_s[:, 1, 0:1], total_, ALU.mult, ALU.add).then_inc(nchain, 1)
                        with dve.Else():
                            dve.sem_inc(nchain, 1)
                        dve.wait_ge(nchain, T.t + (TILES if a == 4 else 0) + 1)
                    else:
                        link(dve.tensor_tensor(prod[:, :, 0:L.out].rearrange("p k (h d) -> p k h d", h=H),
                                               rows[:, :, 0:L.out].rearrange("p k (h d) -> p k h d", h=H),
                                               w_s[:, :, 0:H].unsqueeze(3).to_broadcast([P, 2, H, L.dim]), ALU.mult))
                        link(dve.tensor_tensor(total_, prod[:, 0, 0:L.out], prod[:, 1, 0:L.out], ALU.add))

                    alone(dve)
                    with dve.If(stepped > T.t):
                        n = dve.value_load(sched[0:1, bass.ds(T.t, 1)], min_val=1, max_val=EDGES)
                        done = dve.value_load(sched[0:1, bass.ds(T.t + STEPS, 1)], min_val=0, max_val=EDGES)
                        with dve.Fori(0, n) as j:
                            extra_step(T, done, j)

                X_LINKS = [23, 23, 21, 20, 20]

                def extra_step(T, done, j):
                    here = [0]
                    total_ = total_of(T)
                    link = linker(xchain, total * sum(X_LINKS[:a]) + (done + j) * X_LINKS[a], here)
                    dve.wait_ge(extra_in, (step_base + done + j) * 32 + 32)
                    e = xe_s[:, :, 0:H]
                    m0, m1 = m_s[:, T.par, 0:H], xm_s[:, 0:H]
                    link(dve.tensor_scalar(xmask[:], xslot[:], len_tab[:, bass.ds(T.t, 1), 0:1].rearrange("p t k -> p (t k)"), NONE, ALU.is_ge, ALU.mult))
                    link(dve.tensor_scalar(xslot[:], xslot[:], 2.0, None, ALU.add))
                    link(dve.tensor_tensor(e, extra[:, :, L.out:L.out + H], pair(own_er(T)), ALU.add))
                    link(dve.scalar_tensor_tensor(e, e, SLOPE, e, ALU.mult, ALU.max))
                    link(dve.tensor_tensor(e, e, xmask[:].unsqueeze(2).to_broadcast([P, 2, H]), ALU.add))
                    link(dve.tensor_tensor(m1, xe_s[:, 0, 0:H], m0, ALU.max))
                    link(dve.tensor_tensor(m1, xe_s[:, 1, 0:H], m1, ALU.max))
                    link(dve.tensor_tensor(xdif[:, 0:2, 0:H], e, pair(m1), ALU.subtract))
                    dve.tensor_tensor(xdif[:, 2, 0:H], m0, m1, ALU.subtract).then_inc(xdif_ready, 1)
                    dve.wait_ge(xexp_ready, step_base + done + j + 1)
                    link(dve.tensor_copy(m0, m1))
                    link(dve.tensor_tensor(den[:, 1, 0:H], den[:, 0, 0:H], xp_s[:, 2, 0:H], ALU.mult))
                    link(dve.tensor_tensor(rden[:, 0:H], xp_s[:, 0, 0:H], xp_s[:, 1, 0:H], ALU.add))
                    link(dve.tensor_tensor(den[:, 0, 0:H], den[:, 1, 0:H], rden[:, 0:H], ALU.add))
                    link(dve.reciprocal(rden[:, 0:H], den[:, 0, 0:H]))
                    link(dve.tensor_tensor(xw_s[:, 2, 0:H], den[:, 1, 0:H], rden[:, 0:H], ALU.mult))
                    link(dve.tensor_tensor(xw_s[:, 0:2, 0:H], xp_s[:, 0:2, 0:H], pair(rden[:, 0:H]), ALU.mult))
                    for make in weighted(total_, total_, xw_s[:, 2, 0:H], False):
                        link(make())
                    for k in range(2):
                        for make in weighted(total_, extra[:, k, 0:L.out], xw_s[:, k, 0:H], True):
                            link(make())
                    if L.residual or H == 1:
                        link(dve.tensor_scalar(xw_s[:, 3, 0:H], xw_s[:, 2, 0:H], -1.0, 1.0, ALU.mult, ALU.add))
                    if L.residual:
                        for make in weighted(total_, own_nb[:, T.par, 0, 0:L.out], xw_s[:, 3, 0:H], True):
                            link(make())
                    if H == 1:
                        for make in weighted(total_, bias[:, 0:L.out], xw_s[:, 3, 0:H], True):
                            link(make())
                    dve.sem_inc(extra_used, 1)
                    assert here[0] == X_LINKS[a], (a, here)

                def settle(T, link):
                    v = total_of(T)
                    if norm:
                        link(dve.tensor_tensor(v, v, resid[:, T.par, :], ALU.add))
                    if AFTER[a] == "relu":
                        dve.wait_ge(turned, T.t + base - 1)
                        dve.tensor_tensor(h[:, T.par, 0:L.out], v, bias[:, 0:L.out], ALU.add).then_inc(h_ready, 1)
                        dve.wait_ge(h_ready, T.t + base + 1)
                    elif H > 1:
                        link(dve.tensor_tensor(v, v, bias[:, 0:L.out], ALU.add))
                    if norm:
                        for g in range(2):
                            link(dve.bn_stats(stats[:, g, :], v[:, g * (D // 2):(g + 1) * (D // 2)]))
                        alone(dve)
                        mv, guess = mean_var[:, T.par, :], rstd[:, T.par, 0:1]
                        link(dve.bn_aggr(mv, stats[:].rearrange("p g s -> p (g s)")))
                        link(dve.tensor_scalar(mv[:, 1:2], mv[:, 1:2], LN_EPS, None, ALU.add))
                        link(dve.tensor_scalar(guess, mv[:, 1:2].bitcast(I32), 1, None, ALU.logical_shift_right))
                        dve.tensor_scalar(guess, guess, -1.0, float(RSQRT_BITS), ALU.mult, ALU.add).then_inc(acc_ready, 1)
                    if AFTER[a] == "elu":
                        dve.sem_inc(acc_ready, 1)
                    dve.sem_inc(rows_used, 1)

                def finish(T):
                    v = total_of(T)
                    norms = T.t + TILES * (1 if a == 4 else 0)
                    if AFTER[a] == "elu":
                        dve.wait_ge(elu_ready, T.t + base + 1)
                        if a > 0 or not (isinstance(T.t, int) and T.t < 2):
                            dve.wait_ge(turned, T.t + base - 1)
                        dve.scalar_tensor_tensor(h[:, T.par, 0:D], v, 0.0, expo[:, 0:D], ALU.max, ALU.add).then_inc(h_ready, 1)
                        dve.wait_ge(h_ready, T.t + base + 1)
                    if norm:
                        dve.wait_ge(rstd_ready, norms + 1)
                        if a == 2:
                            dve.wait_ge(turned, T.t + base - 1)
                            if not (isinstance(T.t, int) and T.t < 2):
                                dve.wait_ge(y_out[T.par], T.use * 16)
                        else:
                            dve.wait_ge(y_out[T.par], (T.use + USES[T.par]) * 16)
                        dve.tensor_scalar(normed[:, T.par, :], v, mean_var[:, T.par, 0:1], rstd[:, T.par, 0:1].bitcast(F32), ALU.subtract, ALU.mult).then_inc(normed_ready, 1)
                        dve.wait_ge(normed_ready, norms + 1)
                        if a == 2:
                            dve.sem_inc(h_ready, 1)

                def tile(T):
                    here = [0]
                    link = linker(chain, T.t * per_tile[0] + links_before, here)
                    sums(T, link)
                    settle(T, link)
                    if not (isinstance(T.t, int) and T.t == TILES - 1):
                        scores(T.ahead())
                    if not norm:
                        finish(T)
                    elif not (isinstance(T.t, int) and T.t == 0):
                        finish(T.back(1))
                    per_tile[0] = here[0]

                scores(Tile(0, 0, 0))
                tile_loop(dve, tile, 4, 1)
                if norm:
                    finish(LAST)
                links_before += TILES * per_tile[0]
                for i in range(2):
                    rows_before[i] += rows_a * USES[i]


def ring_uses(cols, j):
    return cols // RING + (1 if j < cols % RING else 0)


_WEIGHTS = ["L0_gnn_W0", "L0_gnn_W1", "L0_gnn_W2", "L1_gnn_W1", "L1_gnn_W2"]
_LEFTS = ["L0_gnn_al0", "L0_gnn_al1", "L0_gnn_al2", "L1_gnn_att_src1", "L1_gnn_att_src2"]
_RIGHTS = ["L0_gnn_ar0", "L0_gnn_ar1", "L0_gnn_ar2", "L1_gnn_att_dst1", "L1_gnn_att_dst2"]
_BIASES = ["L0_gnn_b0", "L0_gnn_b1", "L0_gnn_b2", "L1_gnn_b1", "L1_gnn_b2"]


def kernel(**inputs):
    import numpy as np
    import concourse.bacc as bacc
    from concourse.bass_utils import run_bass_kernel_spmd

    arrays, aps = {}, {}
    nc = bacc.Bacc("TRN2", target_bir_lowering=False, num_devices=1)

    def give(name, a):
        a = np.ascontiguousarray(a)
        arrays["in_" + name] = a
        aps[name] = nc.dram_tensor("in_" + name, a.shape, mybir.dt.from_np(a.dtype), kind="ExternalInput").ap()

    x = np.asarray(inputs["x"])
    x_rows = np.concatenate([x, np.zeros((ROWS - NODES, D), x.dtype)])
    give("x_rows", x_rows)
    give("x_tiles", x_rows.reshape(TILES, P, D // P, P).transpose(0, 3, 2, 1).reshape(TILES, P, D))
    dst, src = np.asarray(inputs["dst"]), np.asarray(inputs["src"])
    far = np.full(EPAD - EDGES + 1, FAR, dst.dtype)
    give("dst_ext", np.concatenate([np.full(1, -1, dst.dtype), dst, far]))
    give("src_ext", np.concatenate([src, np.zeros(EPAD - EDGES + 2, src.dtype)]))
    give("edge_no", np.arange(EPAD, dtype=np.int32).reshape(P, EC))
    node_rows = np.zeros((ROWS, ROW), np.int32)
    node_rows[:, NODE] = np.arange(ROWS)
    give("node_rows", node_rows)
    give("ident", np.eye(P, dtype=np.float32))
    give("before", np.triu(np.ones((P, P), np.float32), 1))
    for name in _WEIGHTS:
        w = np.asarray(inputs[name])
        give(name, w.T if name.startswith("L1") else w)
    for name in _LEFTS + _RIGHTS + _BIASES:
        give(name, np.asarray(inputs[name]).reshape(1, -1))
    out = nc.dram_tensor("out_rows", (ROWS, D), F32, kind="ExternalOutput").ap()
    gat_program(nc, aps["x_tiles"], aps["x_rows"], aps["dst_ext"], aps["src_ext"], aps["edge_no"], aps["node_rows"],
                aps["ident"], aps["before"], [aps[n] for n in _WEIGHTS], [aps[n] for n in _LEFTS],
                [aps[n] for n in _RIGHTS], [aps[n] for n in _BIASES], out)
    r = run_bass_kernel_spmd(nc, [arrays], core_ids=[0])
    return r.results[0]["out_rows"][:NODES]
```

```python
from contextlib import ExitStack

import concourse.bass as bass
from concourse import mybir

ALU = mybir.AluOpType
ACT = mybir.ActivationFunctionType
F32 = mybir.dt.float32
F32R = mybir.dt.float32r
I32 = mybir.dt.int32
AX = mybir.AxisListType.X

P = 128
NODES = 10000
TILES = (NODES + P - 1) // P
ROWS = TILES * P
EDGES = 20000
EC = (EDGES + P - 1) // P
EPAD = EC * P
D = 768
DW = 1024
SLOPE = 0.2
LN_EPS = 1e-5
FAR = 1 << 20
NONE = -2e30
FLOOR = -1e30
RSQRT_BITS = 0x5F3759DF
BUCKETS = 8
RING = 4
START, LEN, SELF, NODE, SRC = 0, 1, 2, 3, 4
ROW = 8
STEPS = TILES
FURTHER, TRIPLE, SEVERAL, SEVERAL_OF = (2 * TILES + k for k in (1, 2, 3, 4))
ZMAX = 1044


class Layer:

    def __init__(self, din, heads, dim, eps, residual):
        self.din, self.heads, self.dim = din, heads, dim
        self.out = heads * dim
        self.kc = din // P
        self.groups = 2 if self.out == D else 3
        self.width = -(-(self.out + 2 * heads) // (2 * self.groups)) * 2 * self.groups
        self.cols = self.width // self.groups
        self.eps, self.residual = eps, residual
        self.size = self.kc * self.width


LAYERS = [Layer(D, 12, 64, 1e-30, True), Layer(D, 12, 64, 1e-30, True), Layer(D, 1, 768, 1e-30, True),
          Layer(D, 8, 128, 1e-16, False), Layer(DW, 1, 768, 1e-16, False)]
SPLIT = (3, 4)
AFTER = ["elu", "elu", "norm_x", "relu", "norm_y"]


class Tile:

    def __init__(self, t, par, use):
        self.t, self.par, self.use = t, par, use

    def ahead(self):
        return Tile(self.t + 1, 1 - self.par, self.use + self.par)

    def back(self, n):
        if n == 0:
            return self
        if (self.par + n) % 2 == self.par:
            return Tile(self.t - n, self.par, self.use - n // 2)
        if self.par == 1:
            return Tile(self.t - n, 0, self.use - (n - 1) // 2)
        return Tile(self.t - n, 1, self.use - (n + 1) // 2)


def tile_loop(eng, body, peel, tail=0):
    for t in range(peel):
        body(Tile(t, t % 2, t // 2))
    pairs = (TILES - peel - tail) // 2
    with eng.Fori(0, pairs) as i:
        for k in range(2):
            par = (peel + k) % 2
            body(Tile(i * 2 + (peel + k), par, i + (peel + k) // 2))
    for t in range(peel + 2 * pairs, TILES):
        body(Tile(t, t % 2, t // 2))


LAST = Tile(TILES - 1, (TILES - 1) % 2, (TILES - 1) // 2)
USES = [(TILES + 1) // 2, TILES // 2]


def gat_program(nc, x_tiles, x_rows, dst_ext, src_ext, edge_no, node_rows, ident_in, before_in,
                weights, lefts, rights, biases, turned_biases, out):
    with ExitStack() as ctx:
        def sb(name, shape, dt=F32):
            return ctx.enter_context(nc.sbuf_tensor(name, shape, dt))

        def sem(name):
            return ctx.enter_context(nc.semaphore(name))

        z_dram = [nc.dram_tensor(f"z{a}_rows", (ROWS, L.width), F32).ap() for a, L in enumerate(LAYERS)]
        y_dram = nc.dram_tensor("y_rows", (ROWS, D), F32).ap()
        node_tab = nc.dram_tensor("node_tab", (ROWS, ROW), I32).ap()
        place_tab = nc.dram_tensor("place_tab", (ROWS, ROW), I32).ap()

        odd = max(LAYERS[0].size + LAYERS[1].size, 2 * LAYERS[3].size)
        even = max(LAYERS[2].size + LAYERS[3].size, 2 * LAYERS[4].size)
        places = {"odd": odd, "even": even, "turned": 4 * DW}
        with ExitStack() as whole_names:
            whole = {n: whole_names.enter_context(nc.sbuf_tensor(f"whole_{n}", [P, size], F32)) for n, size in places.items()}
        halves = {n: sb(f"halves_{n}", [P, size], F32R) for n, size in places.items()}

        def weights_at(names, a, at):
            L = LAYERS[a]
            return names["even" if a in (2, 4) else "odd"][:, at:at + L.size].rearrange("p (c n) -> p c n", c=L.kc)
        w_sb = [weights_at(whole, a, LAYERS[0].size if a == 1 else 0) for a in range(5)]
        w_lo = {a: weights_at(halves, a, 0) for a in SPLIT}
        w_hi = {a: weights_at(halves, a, LAYERS[a].size) for a in SPLIT}
        w_early = {a: whole["even"][:, LAYERS[2].size:LAYERS[2].size + LAYERS[a].size].rearrange(
            "p (c n) -> p c n", c=LAYERS[a].kc) for a in SPLIT}
        early_columns = {a: sb(f"early_columns{a}", [P, LAYERS[a].kc, 2 * LAYERS[a].heads]) for a in SPLIT}

        def turned_at(names, at):
            return names["turned"][:, at:at + 2 * DW].rearrange("p (q n) -> p q n", q=2)
        hT, hT_hi = turned_at(whole, 0), turned_at(halves, 0)
        hT_full, hT_lo = turned_at(whole, 2 * DW), turned_at(halves, 2 * DW)
        near = sb("near", [P, 2, 4, ZMAX])
        acc = sb("acc", [P, 2, DW])
        expo = sb("expo", [P, DW])
        h = sb("h", [P, 2, DW])
        zout = sb("zout", [P, 2, ZMAX])
        bias = sb("bias", [P, D])
        bias_t = sb("bias_t", [P, 3, DW // P])
        resid = sb("resid", [P, 2, D])
        ident = sb("ident", [P, P])
        before = sb("before", [P, P])
        ones = sb("ones", [P, P])

        more = sb("more", [P, 2, ZMAX])
        more_i = more[:].rearrange("p k n -> p (k n)").bitcast(I32)
        dst_i = more_i[:, 0:3 * EC].rearrange("p (k c) -> p k c", k=3)
        src_i = sb("src_i", [P, 3, EC], I32)
        edge_i = sb("edge_i", [P, EC], I32)
        scans = sb("scans", [P, 5, EC])
        erow = more_i[:, 3 * EC:(ROW + 4) * EC].rearrange("p (c k) -> p c k", k=ROW + 1)
        lasts = sb("lasts", [P, 5])
        carried = acc[:, 1, 2 * P:6 * P + 4].rearrange("p (q n) -> p q n", q=4)
        carry = sb("carry", [P, 4])
        counts = sb("counts", [P, 6, BUCKETS])
        rank_f = sb("rank_f", [P, TILES])
        rank_i = sb("rank_i", [P, 2, TILES], I32)
        stage = sb("stage", [P, RING, ROW + 1], I32)
        idx_tab = sb("idx_tab", [P, TILES, 4], I32)
        mask_tab = sb("mask_tab", [P, TILES, 4])
        len_tab = sb("len_tab", [P, TILES, 2])
        sched = sb("sched", [P, 2 * TILES + 6], I32)
        slots = sb("slots", [P, 6])
        gidx = sb("gidx", [P, 2, 4], I32)
        sidx = sb("sidx", [P, 2, 1], I32)
        yidx = sb("yidx", [P, 2, 1], I32)
        gslot = sb("gslot", [P, 2])
        gfar = sb("gfar", [P, 2])
        gedge_f = sb("gedge_f", [P, 2])
        gedge = sb("gedge", [P, 2], I32)
        gsrc = sb("gsrc", [P, 2], I32)
        glen = sb("glen", [P, 2])
        relus = expo
        e_s = sb("e_s", [P, 4, 12])
        m_s = sb("m_s", [P, 2, 12])
        dif = sb("dif", [P, 2, 4, 12])
        p_s = sb("p_s", [P, 2, 4, 12])
        half = sb("half", [P, 2, 12])
        den = sb("den", [P, 2, 12])
        rden = sb("rden", [P, 12])
        w_s = sb("w_s", [P, 4, 12])
        xe_s = sb("xe_s", [P, 2, 12])
        xm_s = sb("xm_s", [P, 12])
        xdif = sb("xdif", [P, 3, 12])
        xp_s = sb("xp_s", [P, 3, 12])
        xw_s = sb("xw_s", [P, 4, 12])
        xslot = sb("xslot", [P, 2])
        xmask = sb("xmask", [P, 2])
        stats = sb("stats", [P, 2, 6])
        mean_var = sb("mean_var", [P, 2, 2])
        rstd = sb("rstd", [P, 2, 4], I32)

        leftright = [near[:, 0, 0:2], near[:, 0, 2:4], near[:, 1, 0:2], h, resid]
        onehot = near[:, 1, 2, 0:BUCKETS * TILES]
        running = near[:, 1, 3, 0:BUCKETS * TILES]
        zeros = acc[:, 0, 0:EC]
        across = acc[:, 0, 2 * P:7 * P]
        most = scans[:, 0:2, :].rearrange("p q c -> p (q c)")
        erow_flat = erow[:].rearrange("p c k -> p (c k)")
        nload_flat = erow_flat[:, 0:TILES * ROW]
        nload = nload_flat.rearrange("p (c k) -> p c k", k=ROW)
        nrow = erow_flat[:, TILES * ROW:TILES * (2 * ROW + 1)].rearrange("p (c k) -> p c k", k=ROW + 1)
        one_row = expo[:, 0:BUCKETS * TILES]
        keep = expo[:, BUCKETS * TILES:BUCKETS * TILES + EC]
        etmp = acc[:, 1, 0:EC]
        wprod = acc[:, 0, :]

        zps = ctx.enter_context(nc.psum_tensor("zps", [P, 2, 3, 512], F32))
        tps = ctx.enter_context(nc.psum_tensor("tps", [P, 1024], F32))

        edges_in = sem("edges_in")
        consts_in = sem("consts_in")
        rows_in = sem("rows_in")
        bias_t_in = sem("bias_t_in")
        w_in = [sem(f"w_in{a}") for a in range(5)]
        sides_in = [sem(f"sides_in{a}") for a in range(5)]
        early_in = {a: sem(f"early_in{a}") for a in SPLIT}
        early_used = sem("early_used")
        x_in = [sem(f"x_in{i}") for i in range(2)]
        z0_out = [sem(f"z0_out{i}") for i in range(2)]
        bias_in = sem("bias_in")
        fchain = sem("fchain")
        slot_chain = sem("slot_chain")
        nchain = sem("nchain")
        schain = sem("schain")
        wchain = sem("wchain")
        chain = sem("chain")
        xchain = sem("xchain")
        gcopied = sem("gcopied")
        scopied = sem("scopied")
        ycopied = sem("ycopied")
        gchain = sem("gchain")
        achain = sem("achain")
        w_ready = sem("w_ready")
        lasts_ready = sem("lasts_ready")
        lasts_turned = sem("lasts_turned")
        carry_ready = sem("carry_ready")
        carry_turned = sem("carry_turned")
        staged = sem("staged")
        ring_out = [sem(f"ring_out{i}") for i in range(RING)]
        nodes_in = sem("nodes_in")
        places_in = sem("places_in")
        counted = sem("counted")
        counts_summed = sem("counts_summed")
        lens_ready = sem("lens_ready")
        lens_turned = sem("lens_turned")
        most_ready = sem("most_ready")
        most_turned = sem("most_turned")
        tables_ready = sem("tables_ready")
        waits_met = sem("waits_met")
        resid_in = [sem(f"resid_in{i}") for i in range(2)]
        gathered = [sem(f"gathered{i}") for i in range(2)]
        rows_used = sem("rows_used")
        dif_ready = sem("dif_ready")
        exp_ready = sem("exp_ready")
        xdif_ready = sem("xdif_ready")
        xexp_ready = sem("xexp_ready")
        gathered_more = [sem(f"gathered_more{i}") for i in range(2)]
        hi_ready = sem("hi_ready")
        tps_read = sem("tps_read")
        extra_in = sem("extra_in")
        extra_used = sem("extra_used")
        src_in = sem("src_in")
        acc_ready = sem("acc_ready")
        elu_ready = sem("elu_ready")
        summed = sem("summed")
        h_ready = sem("h_ready")
        normed_ready = sem("normed_ready")
        turned = sem("turned")
        hT_ready = sem("hT_ready")
        mm_done = sem("mm_done")
        z_ready = sem("z_ready")
        z_out = [sem(f"z_out{i}") for i in range(2)]
        y_out = [sem(f"y_out{i}") for i in range(2)]

        block = ctx.enter_context(nc.Block())

        def alone(eng):
            eng.sem_inc(waits_met, 1)

        def heads_of(ap, L):
            return ap.rearrange("p (h d) -> p h d", h=L.heads)

        def over_dim(ap, L):
            return ap.unsqueeze(2).to_broadcast([P, L.heads, L.dim])

        @block.sync
        def _(sp):
            for k in range(3):
                sp.dma_start(dst_i[:, k, :], dst_ext[k:k + EPAD].rearrange("(p c) -> p c", c=EC)).then_inc(edges_in, 16)
                sp.dma_start(src_i[:, k, :], src_ext[k:k + EPAD].rearrange("(p c) -> p c", c=EC)).then_inc(edges_in, 16)
            sp.dma_start(edge_i[:], edge_no).then_inc(edges_in, 16)
            sp.dma_start(ident[:], ident_in).then_inc(consts_in, 16)
            sp.dma_start(before[:], before_in).then_inc(consts_in, 16)
            sp.dma_start(node_tab, node_rows).then_inc(rows_in, 16)

            def load_weights(a):
                L = LAYERS[a]
                sp.dma_start(w_sb[a][:, :, 0:L.out], weights[a].rearrange("(c p) n -> p c n", p=P)).then_inc(w_in[a], 16)

            def load_sides(a):
                L = LAYERS[a]
                sp.dma_start(leftright[a][:, 0, 0:L.out], lefts[a].to_broadcast([P, L.out])).then_inc(sides_in[a], 16)
                sp.dma_start(leftright[a][:, 1, 0:L.out], rights[a].to_broadcast([P, L.out])).then_inc(sides_in[a], 16)

            for k, a in enumerate(a for a in range(5) if not AFTER[a].startswith("norm")):
                sp.dma_start(bias_t[:, k, 0:LAYERS[a].out // P], turned_biases[k]).then_inc(bias_t_in, 16)

            def load_bias(a):
                L = LAYERS[a]
                sp.dma_start(bias[:], biases[a].to_broadcast([P, L.out])).then_inc(bias_in, 16)

            for a in range(3):
                load_weights(a)
                load_sides(a)
            load_bias(2)
            early, later = SPLIT
            sp.dma_start(w_early[early][:, :, 0:LAYERS[early].out], weights[early].rearrange("(c p) n -> p c n", p=P)).then_inc(early_in[early], 16)
            load_sides(early)
            load_sides(later)

            def store_z0(T):
                sp.wait_ge(z_ready, T.t + 1)
                sp.dma_start(z_dram[0].rearrange("(t p) n -> t p n", p=P)[bass.ds(T.t, 1)].rearrange("t p n -> (t p) n"),
                             zout[:, T.par, 0:LAYERS[0].width]).then_inc(z0_out[T.par], 16)

            def move(T):
                if not (isinstance(T.t, int) and T.t < 2):
                    sp.wait_ge(mm_done, T.t - 1)
                sp.dma_start(hT[:, T.par, 0:D], x_tiles[bass.ds(T.t, 1)].rearrange("t p n -> (t p) n")).then_inc(x_in[T.par], 16)
                if not (isinstance(T.t, int) and T.t < 2):
                    store_z0(T.back(2))

            tile_loop(sp, move, 3)
            store_z0(LAST.back(1))
            store_z0(LAST)
            for a in SPLIT:
                sp.wait_ge(mm_done, TILES * (a - 1))
                load_weights(a)
            sp.wait_ge(rows_used, TILES * 3)
            load_bias(4)

        @block.tensor
        def _(pe):
            def products(a, T):
                L = LAYERS[a]
                for g in range(L.groups):
                    if a in SPLIT:
                        cols = slice(g * L.cols, (g + 1) * L.cols)
                        for c in range(L.kc):
                            s = slice(c * P, (c + 1) * P)
                            lo, hi = hT_lo[:, T.par, s], hT_hi[:, T.par, s]
                            wlo, whi = w_lo[a][:, c, cols], w_hi[a][:, c, cols]
                            for k, (left, right) in enumerate([(lo, whi), (hi, wlo), (hi, whi)]):
                                mm = pe.matmul(zps[:, T.par, g, 0:L.cols], left, right,
                                               start=(c == 0 and k == 0), stop=(c == L.kc - 1 and k == 2))
                        continue
                    for c in range(L.kc):
                        mm = pe.matmul(zps[:, T.par, g, 0:L.cols], hT[:, T.par, c * P:(c + 1) * P],
                                       w_sb[a][:, c, g * L.cols:(g + 1) * L.cols],
                                       start=(c == 0), stop=(c == L.kc - 1))
                mm.then_inc(mm_done, 1)

            def first_layer(T):
                pe.wait_ge(x_in[T.par], (T.use + 1) * 16)
                if not (isinstance(T.t, int) and T.t < 2):
                    pe.wait_ge(z_ready, T.t - 1)
                products(0, T)

            pe.wait_ge(consts_in, 32)
            pe.wait_ge(lasts_ready, 1)
            for q in range(5):
                turn = pe.transpose(tps[0:1, q * P:(q + 1) * P], lasts[:, q:q + 1], ident[:])
            turn.then_inc(lasts_turned, 1)
            pe.wait_ge(carry_ready, 1)
            for q in range(4):
                turn = pe.transpose(tps[:, 640 + q:641 + q], carried[0:1, q, 0:P], ident[0:1, 0:1])
            turn.then_inc(carry_turned, 1)
            pe.wait_ge(w_ready, 1)
            first_sums, second_sums = TILES * 5 // 16, TILES * 11 // 16
            first_layer(Tile(0, 0, 0))
            first_layer(Tile(1, 1, 0))
            first_layer(Tile(2, 0, 1))
            with pe.Fori(1, first_sums // 2) as i:
                first_layer(Tile(i * 2 + 1, 1, i))
                first_layer(Tile(i * 2 + 2, 0, i + 1))
            pe.wait_ge(counted, 1)
            pe.matmul(tps[:, 0:BUCKETS], before[:], counts[:, 0, :], start=True, stop=True)
            pe.matmul(tps[:, 512:512 + BUCKETS], ones[:], counts[:, 0, :], start=True, stop=True).then_inc(counts_summed, 1)
            with pe.Fori(first_sums // 2, second_sums // 2) as i:
                first_layer(Tile(i * 2 + 1, 1, i))
                first_layer(Tile(i * 2 + 2, 0, i + 1))
            pe.wait_ge(lens_ready, 1)
            pe.transpose(tps[0:TILES, 0:P], len_tab[:, :, 0], ident[:]).then_inc(lens_turned, 1)
            pe.wait_ge(most_ready, 1)
            pe.transpose(tps[0:1, 512:512 + TILES], most[0:TILES, 0:1], ident[0:TILES, 0:TILES]).then_inc(most_turned, 1)
            with pe.Fori(second_sums // 2, TILES // 2) as i:
                first_layer(Tile(i * 2 + 1, 1, i))
                first_layer(Tile(i * 2 + 2, 0, i + 1))
            pe.wait_ge(tables_ready, 1)

            for a in range(1, 5):
                L = LAYERS[a]
                base = (a - 1) * TILES

                def turn_h(T):
                    pe.wait_ge(h_ready, T.t + base + 1)
                    if not (isinstance(T.t, int) and T.t + base == 0):
                        pe.wait_ge(tps_read, T.t + base)
                    for c in range(L.kc):
                        turn = pe.transpose(tps[:, c * P:(c + 1) * P], h[:, T.par, c * P:(c + 1) * P], ident[:])
                    turn.then_inc(turned, 1)

                def multiply(T):
                    pe.wait_ge(hT_ready, T.t + base + 1)
                    pe.wait_ge(z_ready, T.t + a * TILES - 1)
                    products(a, T)

                def step(T):
                    turn_h(T)
                    if not isinstance(T.t, int):
                        multiply(T.back(1))

                if a in SPLIT:
                    pe.wait_ge(w_ready, a - 1)
                tile_loop(pe, step, 1)
                multiply(LAST)

            def residual_and_bias(T):
                pe.wait_ge(rows_used, T.t + 4 * TILES - 1)
                halves = [slice(g * (D // 2), (g + 1) * (D // 2)) for g in range(2)]
                for g, s in enumerate(halves):
                    pe.matmul(zps[:, T.par, g, 0:D // 2], ones[0:1, :], bias[0:1, s], start=True, stop=False)
                pe.wait_ge(resid_in[T.par], (T.use + (USES[T.par] + 1)) * 16)
                for g, s in enumerate(halves):
                    mm = pe.matmul(zps[:, T.par, g, 0:D // 2], ident[:], resid[:, T.par, s], start=False, stop=True)
                mm.then_inc(summed, 1)

            pe.wait_ge(z_ready, 5 * TILES)
            pe.wait_ge(bias_in, 32)
            tile_loop(pe, residual_and_bias, 1)

        @block.scalar
        def _(act):
            def take_z(a, T):
                L = LAYERS[a]
                act.wait_ge(mm_done, T.t + a * TILES + 1)
                act.activation(zout[:, T.par, 0:L.width].rearrange("p (g n) -> p g n", g=L.groups),
                               zps[:, T.par, 0:L.groups, 0:L.cols], ACT.Copy).then_inc(z_ready, 1)

            def first_layer(T):
                if not (isinstance(T.t, int) and T.t < 2):
                    act.wait_ge(z0_out[T.par], T.use * 16)
                take_z(0, T)

            tile_loop(act, first_layer, 3)
            act.wait_ge(tables_ready, 1)
            for a in range(5):
                L = LAYERS[a]
                norm = AFTER[a].startswith("norm")
                base = a * TILES
                further = act.value_load(sched[0:1, FURTHER:FURTHER + 1], min_val=0, max_val=TILES)
                total = act.value_load(sched[0:1, STEPS + TILES:STEPS + TILES + 1], min_val=0, max_val=EDGES)
                step_base = total * a

                def weigh(T):
                    act.wait_ge(dif_ready, T.t + base + 1)
                    act.activation(p_s[:, T.par, :, 0:L.heads], dif[:, T.par, :, 0:L.heads], ACT.Exp).then_inc(exp_ready, 1)

                def weigh_extra(T):
                    with act.If(further > T.t):
                        n = act.value_load(sched[0:1, bass.ds(T.t, 1)], min_val=1, max_val=EDGES)
                        done = act.value_load(sched[0:1, bass.ds(T.t + STEPS, 1)], min_val=0, max_val=EDGES)
                        with act.Fori(0, n) as j:
                            act.wait_ge(xdif_ready, step_base + done + j + 1)
                            act.activation(xp_s[:, :, 0:L.heads], xdif[:, :, 0:L.heads], ACT.Exp).then_inc(xexp_ready, 1)

                def finish(T):
                    if AFTER[a].startswith("norm"):
                        norms = (TILES * (1 if a == 4 else 0)) + T.t
                        act.wait_ge(acc_ready, norms + 1)
                        v = mean_var[:, T.par, 1:2]
                        y, y2, vy2, c = (rstd[:, T.par, k:k + 1].bitcast(F32) for k in range(4))
                        at = norms * 14 + 2 * TILES
                        for k in range(3):
                            steps = [lambda: act.activation(y2, y, ACT.Square),
                                     lambda: act.activation(vy2, y2, ACT.Copy, scale=v),
                                     lambda: act.activation(c, vy2, ACT.Identity, scale=-0.5, bias=slots[:, 4:5]),
                                     lambda: act.activation(y, c, ACT.Copy, scale=y)]
                            for m, make in enumerate(steps):
                                make().then_inc(achain, 1)
                                act.wait_ge(achain, at + (4 * k + m + 1))
                        act.activation(y2, mean_var[:, T.par, 0:1], ACT.Copy, scale=y).then_inc(achain, 1)
                        act.wait_ge(achain, at + 13)
                        act.activation(vy2, y2, ACT.Copy, scale=-1.0).then_inc(achain, 1)
                        act.wait_ge(achain, at + 14)
                        if a == 2:
                            act.wait_ge(turned, T.t + base - 1)
                            if not (isinstance(T.t, int) and T.t < 2):
                                act.wait_ge(y_out[T.par], T.use * 16)
                        else:
                            act.wait_ge(y_out[T.par], (T.use + USES[T.par]) * 16)
                        act.activation(h[:, T.par, 0:D], acc[:, T.par, 0:D], ACT.Identity, scale=y, bias=vy2).then_inc(normed_ready, 1)
                        act.wait_ge(normed_ready, norms + 1)
                        if a == 2:
                            act.sem_inc(h_ready, 1)

                def take_h(T):
                    M = LAYERS[a + 1]
                    act.wait_ge(turned, T.t + base + 1)
                    act.wait_ge(mm_done, T.t + (a + 1) * TILES - 1)
                    full = hT_full if a + 1 in SPLIT else hT
                    if norm:
                        act.activation(full[:, T.par, 0:M.din], tps[:, 0:M.din], ACT.Copy).then_inc(tps_read, 1)
                    else:
                        func, k = (ACT.Relu, 2) if AFTER[a] == "relu" else (ACT.Identity, a)
                        for c in range(M.kc):
                            s = slice(c * P, (c + 1) * P)
                            ins = act.activation(full[:, T.par, s], tps[:, s], func, bias=bias_t[:, k, c:c + 1])
                        ins.then_inc(tps_read, 1)
                    if a + 1 in SPLIT:
                        act.wait_ge(tps_read, T.t + base + 1)
                        act.activation(hT_hi[:, T.par, 0:M.din], full[:, T.par, 0:M.din], ACT.Copy).then_inc(hi_ready, 1)
                    if AFTER[a] == "elu":
                        elus = T.t + base
                        act.wait_ge(tps_read, elus + 1)
                        if not (isinstance(T.t, int) and elus == 0):
                            act.wait_ge(hT_ready, elus)
                        act.activation(relus[:, 0:D], hT[:, T.par, 0:D], ACT.Relu, scale=-1.0, bias=slots[:, 5:6]).then_inc(achain, 1)
                        act.wait_ge(achain, elus + 1)
                        act.activation(expo[:, 0:D], relus[:, 0:D], ACT.Exp, scale=-1.0).then_inc(elu_ready, 1)

                def free_and_take_z(T, first_two):
                    if not first_two:
                        act.wait_ge(z_out[T.par], (USES[T.par] * a + T.use) * 16)
                    take_z(a + 1, T)

                late = 1 if norm else 0

                def step(T):
                    weigh_extra(T)
                    if not (isinstance(T.t, int) and T.t == TILES - 1):
                        weigh(T.ahead())
                    if norm:
                        finish(T)
                    if a < 4:
                        if not (isinstance(T.t, int) and T.t < late):
                            take_h(T.back(late))
                        if not (isinstance(T.t, int) and T.t < 2 + late):
                            free_and_take_z(T.back(2 + late), isinstance(T.t, int) and T.t < 4 + late)

                weigh(Tile(0, 0, 0))
                tile_loop(act, step, 5, 1)
                if a < 4:
                    if late:
                        take_h(LAST)
                        free_and_take_z(LAST.back(2), False)
                    free_and_take_z(LAST.back(1), False)
                    free_and_take_z(LAST, False)

        @block.gpsimd
        def _(pool):
            def scatter(ncols, before_cols, table):
                def column(c, j):
                    pool.wait_ge(staged, c + before_cols + 1)
                    alone(pool)
                    pool.indirect_dma_start(
                        out=table, out_offset=bass.IndirectOffsetOnAxis(ap=stage[:, j, ROW:ROW + 1], axis=0),
                        in_=stage[:, j, 0:ROW], in_offset=None, bounds_check=ROWS - 1, oob_is_err=False,
                    ).then_inc(ring_out[j], 16)
                with pool.Fori(0, ncols // RING) as r:
                    for j in range(RING):
                        column(r * RING + j, j)
                for j in range(ncols % RING):
                    column(ncols // RING * RING + j, j)

            pool.wait_ge(rows_in, 16)
            scatter(EC, 0, node_tab)
            for j in range(RING):
                pool.wait_ge(ring_out[j], 16 * ring_uses(EC, j))
            pool.dma_start(nload_flat, node_tab.rearrange("(p c) k -> p (c k)", p=P)).then_inc(nodes_in, 16)
            scatter(TILES, EC, place_tab)
            for j in range(RING):
                pool.wait_ge(ring_out[j], 16 * (ring_uses(EC, j) + ring_uses(TILES, j)))
            pool.dma_start(nload_flat, place_tab.rearrange("(p c) k -> p (c k)", p=P)).then_inc(places_in, 16)
            pool.wait_ge(tables_ready, 1)
            a = SPLIT[1]
            pool.wait_ge(early_used, 1)
            pool.dma_start(w_early[a][:, :, 0:LAYERS[a].out], weights[a].rearrange("(c p) n -> p c n", p=P)).then_inc(early_in[a], 16)

            def rows_of(table, target, index, signal):
                pool.indirect_dma_start(
                    out=target, out_offset=None, in_=table,
                    in_offset=bass.IndirectOffsetOnAxis(ap=index, axis=0),
                    bounds_check=ROWS - 1, oob_is_err=False).then_inc(signal, 16)

            def to_rows(table, source, index, signal):
                pool.indirect_dma_start(
                    out=table, out_offset=bass.IndirectOffsetOnAxis(ap=index, axis=0),
                    in_=source, in_offset=None, bounds_check=ROWS - 1, oob_is_err=False).then_inc(signal, 16)

            for a in range(5):
                L = LAYERS[a]
                norm = AFTER[a].startswith("norm")
                base = a * TILES
                norms = TILES * (1 if a == 4 else 0)
                for i in range(2):
                    if a == 0:
                        pool.wait_ge(z0_out[i], 16 * USES[i])
                    else:
                        pool.wait_ge(z_out[i], 16 * USES[i] * a)
                    if a == 4:
                        pool.wait_ge(y_out[i], 16 * USES[i])
                further = pool.value_load(sched[0:1, FURTHER:FURTHER + 1], min_val=0, max_val=TILES)
                several = pool.value_load(sched[0:1, SEVERAL:SEVERAL + 1], min_val=0, max_val=TILES)
                total = pool.value_load(sched[0:1, STEPS + TILES:STEPS + TILES + 1], min_val=0, max_val=EDGES)
                step_base = total * a

                def fetch(T):
                    if isinstance(T.t, int) and T.t < 2:
                        if a:
                            pool.wait_ge(rows_used, base)
                    else:
                        pool.wait_ge(rows_used, T.t + base - 1)
                        alone(pool)
                    pool.tensor_copy(gidx[:, T.par, :], idx_tab[:, bass.ds(T.t, 1), :].rearrange("p t k -> p (t k)")).then_inc(gcopied, 1)
                    pool.tensor_copy(glen[:], len_tab[:, bass.ds(T.t, 1), :].rearrange("p t k -> p (t k)")).then_inc(gcopied, 1)
                    pool.tensor_copy(gslot[:], slots[:, 2:4]).then_inc(gcopied, 1)
                    pool.wait_ge(gcopied, (T.t + base + 1) * 3)
                    alone(pool)
                    if norm:
                        rows_of(x_rows if a == 2 else y_dram, resid[:, T.par, :], gidx[:, T.par, 0:1], resid_in[T.par])
                    for k in range(2):
                        rows_of(z_dram[a], near[:, T.par, k, 0:L.width], gidx[:, T.par, k:k + 1], gathered[T.par])
                    with pool.If(several > T.t):
                        for k in (2, 3):
                            rows_of(z_dram[a], near[:, T.par, k, 0:L.width], gidx[:, T.par, k:k + 1], gathered_more[T.par])

                def fetch_further(T):
                    with pool.If(further > T.t):
                        n = pool.value_load(sched[0:1, bass.ds(T.t, 1)], min_val=1, max_val=EDGES)
                        done = pool.value_load(sched[0:1, bass.ds(T.t + STEPS, 1)], min_val=0, max_val=EDGES)
                        with pool.Fori(0, n) as j:
                            g = step_base + done + j
                            pool.tensor_scalar(gfar[:], gslot[:], glen[:, 0:1], float(FAR), ALU.is_ge, ALU.mult).then_inc(gchain, 1)
                            pool.tensor_scalar(gedge_f[:], gslot[:], glen[:, 1:2], None, ALU.add).then_inc(gchain, 1)
                            pool.memset(gsrc[:], FAR).then_inc(gchain, 1)
                            pool.wait_ge(gchain, g * 6 + 3)
                            alone(pool)
                            pool.tensor_tensor(gedge_f[:], gedge_f[:], gfar[:], ALU.add).then_inc(gchain, 1)
                            pool.tensor_scalar(gslot[:], gslot[:], 2.0, None, ALU.add).then_inc(gchain, 1)
                            pool.wait_ge(gchain, g * 6 + 5)
                            alone(pool)
                            pool.tensor_copy(gedge[:], gedge_f[:]).then_inc(gchain, 1)
                            pool.wait_ge(gchain, g * 6 + 6)
                            alone(pool)
                            for k in range(2):
                                pool.indirect_dma_start(
                                    out=gsrc[:, k:k + 1], out_offset=None, in_=src_ext.rearrange("(n o) -> n o", o=1),
                                    in_offset=bass.IndirectOffsetOnAxis(ap=gedge[:, k:k + 1], axis=0),
                                    bounds_check=EDGES - 1, oob_is_err=False).then_inc(src_in, 16)
                            pool.wait_ge(src_in, g * 32 + 32)
                            alone(pool)
                            pool.wait_ge(extra_used, g + 1)
                            alone(pool)
                            for k in range(2):
                                rows_of(z_dram[a], more[:, k, 0:L.width], gsrc[:, k:k + 1], extra_in)
                            pool.wait_ge(extra_in, g * 32 + 32)
                            alone(pool)

                def spread_z(T):
                    pool.wait_ge(z_ready, T.t + base + TILES + 1)
                    alone(pool)
                    pool.tensor_copy(sidx[:, T.par, :], idx_tab[:, bass.ds(T.t, 1), 0:1].rearrange("p t k -> p (t k)")).then_inc(scopied, 1)
                    pool.wait_ge(scopied, T.t + base + 1)
                    alone(pool)
                    to_rows(z_dram[a + 1], zout[:, T.par, 0:LAYERS[a + 1].width], sidx[:, T.par, :], z_out[T.par])

                def spread_y(T):
                    pool.wait_ge(normed_ready, T.t + norms + 1)
                    alone(pool)
                    pool.tensor_copy(yidx[:, T.par, :], idx_tab[:, bass.ds(T.t, 1), 0:1].rearrange("p t k -> p (t k)")).then_inc(ycopied, 1)
                    pool.wait_ge(ycopied, T.t + norms + 1)
                    alone(pool)
                    to_rows(y_dram if a == 2 else out, h[:, T.par, 0:D], yidx[:, T.par, :], y_out[T.par])

                lag = 6 if norm else 5

                def step(T):
                    fetch(T)
                    fetch_further(T)
                    if norm and not (isinstance(T.t, int) and T.t < 3):
                        spread_y(T.back(3))
                    if a < 4 and not (isinstance(T.t, int) and T.t < lag):
                        spread_z(T.back(lag))

                tile_loop(pool, step, lag)
                if norm:
                    for n in (2, 1, 0):
                        spread_y(LAST.back(n))
                if a < 4:
                    for n in range(lag - 1, -1, -1):
                        spread_z(LAST.back(n))
            for i in range(2):
                pool.wait_ge(y_out[i], 16 * 2 * USES[i])

        @block.vector
        def _(dve):
            chained = [0]

            def link(ins):
                ins.then_inc(chain, 1)
                chained[0] += 1
                dve.wait_ge(chain, chained[0])

            link(dve.memset(acc[:], 0.0))
            link(dve.memset(one_row[:], 1.0))
            link(dve.memset(ones[:], 1.0))
            link(dve.memset(carried[:], 0.0))
            for k in range(4):
                link(dve.memset(slots[:, k:k + 1], float(k + 1)))
            link(dve.memset(slots[:, 4:5], 1.5))
            link(dve.memset(slots[:, 5:6], -1.0))
            for a, L in enumerate(LAYERS[:3]):
                used = L.out + 2 * L.heads
                if used < L.width:
                    link(dve.memset(w_sb[a][:, :, used:L.width], 0.0))
            dve.wait_ge(edges_in, 16 * 7)
            prv, dst, nxt = dst_i[:, 0, :], dst_i[:, 1, :], dst_i[:, 2, :]
            link(dve.tensor_tensor(keep[:], dst, prv, ALU.is_equal))
            link(dve.tensor_tensor_scan(scans[:, 0, :], keep[:], zeros, 1.0, ALU.mult, ALU.add))
            for q in range(4):
                said = edge_i[:] if q == 0 else src_i[:, q - 1, :]
                link(dve.tensor_tensor(etmp[:], said, keep[:], ALU.mult))
                link(dve.tensor_tensor(etmp[:], said, etmp[:], ALU.subtract))
                link(dve.tensor_tensor_scan(scans[:, q + 1, :], keep[:], etmp[:], 0.0, ALU.mult, ALU.add))
            dve.tensor_copy(lasts[:], scans[:, :, EC - 1]).then_inc(lasts_ready, 1)
            dve.wait_ge(lasts_turned, 1)
            link(dve.tensor_copy(across[0:1, :], tps[0:1, 0:5 * P]))
            for q in range(4):
                scan = dve.tensor_tensor_scan(carried[0:1, q, 1:P + 1], across[0:1, 0:P],
                                              across[0:1, (q + 1) * P:(q + 2) * P], 0.0, ALU.mult, ALU.add)
                if q < 3:
                    link(scan)
            scan.then_inc(carry_ready, 1)
            dve.wait_ge(carry_ready, 1)
            dve.wait_ge(carry_turned, 1)
            link(dve.tensor_copy(carry[:], tps[:, 640:644]))
            for q in range(4):
                link(dve.scalar_tensor_tensor(scans[:, q + 1, :], scans[:, 0, :], carry[:, q:q + 1],
                                              scans[:, q + 1, :], ALU.mult, ALU.add))
            link(dve.tensor_copy(erow[:, :, START], scans[:, 1, :]))
            link(dve.tensor_copy(erow[:, :, NODE], dst))
            for k in range(3):
                link(dve.tensor_copy(erow[:, :, SRC + k], scans[:, 2 + k, :]))
            link(dve.memset(erow[:, :, ROW - 1:ROW], 0))
            link(dve.tensor_tensor(etmp[:], src_i[:, 0, :], dst, ALU.is_equal))
            link(dve.tensor_copy(erow[:, :, SELF], etmp[:]))
            link(dve.tensor_tensor(etmp[:], edge_i[:], etmp[:], ALU.subtract))
            link(dve.scalar_tensor_tensor(erow[:, :, LEN], etmp[:], 1.0, scans[:, 1, :], ALU.add, ALU.subtract))
            link(dve.tensor_tensor(etmp[:], dst, nxt, ALU.is_equal))
            link(dve.scalar_tensor_tensor(erow[:, :, ROW], etmp[:], float(FAR), dst, ALU.mult, ALU.add))

            wchained = [0]

            def wlink(ins, at):
                ins.then_inc(wchain, 1)
                dve.wait_ge(wchain, at)

            def score_columns(a):
                L = LAYERS[a]
                dve.wait_ge(sides_in[a], 32)
                if a in SPLIT:
                    dve.wait_ge(early_in[a], 16)
                    products, w_all, columns = expo, w_early[a], early_columns[a]
                else:
                    dve.wait_ge(w_in[a], 16)
                    products, w_all, columns = wprod, w_sb[a], w_sb[a][:, :, L.out:L.out + 2 * L.heads]
                with dve.Fori(0, L.kc) as c:
                    for side in range(2):
                        w = w_all[:, bass.ds(c, 1), 0:L.out].rearrange("p t n -> p (t n)")
                        column = columns[:, bass.ds(c, 1), side * L.heads:(side + 1) * L.heads].rearrange("p t n -> p (t n)")
                        at = c * 4 + (wchained[0] + side * 2)
                        wlink(dve.tensor_tensor(products[:, 0:L.out], w, leftright[a][:, side, 0:L.out], ALU.mult), at + 1)
                        wlink(dve.tensor_reduce(column, heads_of(products[:, 0:L.out], L), AX, ALU.add), at + 2)
                wchained[0] += 4 * L.kc

            def split_weights(a):
                L = LAYERS[a]
                dve.wait_ge(w_in[a], 16)
                flat = lambda w: w.rearrange("p c n -> p (c n)")
                used = L.out + 2 * L.heads
                wlink(dve.memset(w_sb[a][:, :, used:L.width], 0.0), wchained[0] + 1)
                wlink(dve.tensor_copy(w_sb[a][:, :, L.out:used], early_columns[a][:]), wchained[0] + 2)
                wlink(dve.tensor_copy(flat(w_hi[a]), flat(w_sb[a])), wchained[0] + 3)
                dve.tensor_tensor(flat(w_lo[a]), flat(w_sb[a]), flat(w_hi[a]).bitcast(F32), ALU.subtract).then_inc(w_ready, 1)
                wchained[0] += 3

            score_columns(0)
            dve.sem_inc(w_ready, 1)

            def stage_rows(source, ncols, before_cols):
                def column(c, j, turn):
                    if not (isinstance(turn, int) and turn == 0):
                        dve.wait_ge(ring_out[j], turn * 16)
                    dve.tensor_copy(stage[:, j, :], source[:, bass.ds(c, 1), :].rearrange("p t k -> p (t k)")).then_inc(staged, 1)
                earlier = [ring_uses(before_cols, j) for j in range(RING)]
                for j in range(RING):
                    column(j, j, earlier[j])
                with dve.Fori(1, ncols // RING) as r:
                    for j in range(RING):
                        column(r * RING + j, j, r + earlier[j])
                for j in range(ncols % RING):
                    column(ncols // RING * RING + j, j, ncols // RING + earlier[j])

            stage_rows(erow, EC, 0)

            dve.wait_ge(nodes_in, 16)
            link(dve.tensor_copy(nrow[:, :, 0:ROW], nload[:]))
            for k in range(BUCKETS):
                link(dve.tensor_scalar(onehot[:, k * TILES:(k + 1) * TILES], nload[:, :, LEN], float(BUCKETS - 1),
                                       float(BUCKETS - 1 - k), ALU.min, ALU.is_equal))
            dve.tensor_reduce(counts[:, 0, :], onehot.rearrange("p (k c) -> p k c", k=BUCKETS), AX, ALU.add).then_inc(counted, 1)
            link(dve.tensor_tensor_scan(running, one_row[:, 0:BUCKETS * TILES], onehot, 0.0, ALU.mult, ALU.add))
            dve.wait_ge(counted, 1)
            dve.wait_ge(counts_summed, 1)
            link(dve.tensor_copy(counts[:, 1, :], tps[:, 0:BUCKETS]))
            link(dve.tensor_copy(counts[:, 2, :], tps[:, 512:512 + BUCKETS]))
            link(dve.tensor_tensor_scan(counts[:, 3, :], one_row[:, 0:BUCKETS], counts[:, 2, :], 0.0, ALU.mult, ALU.add))
            link(dve.tensor_tensor_scan(counts[:, 4, :], one_row[:, 0:BUCKETS], counts[:, 0, :], 0.0, ALU.mult, ALU.add))
            link(dve.tensor_tensor(counts[:, 3, :], counts[:, 3, :], counts[:, 2, :], ALU.subtract))
            link(dve.tensor_tensor(counts[:, 4, :], counts[:, 4, :], counts[:, 0, :], ALU.subtract))
            link(dve.tensor_tensor(counts[:, 3, :], counts[:, 3, :], counts[:, 1, :], ALU.add))
            link(dve.tensor_tensor(counts[:, 5, :], counts[:, 3, :], counts[:, 4, :], ALU.subtract))
            for k in range(BUCKETS):
                s = slice(k * TILES, (k + 1) * TILES)
                link(dve.scalar_tensor_tensor(running[:, s], running[:, s], counts[:, 5, k:k + 1], onehot[:, s],
                                              ALU.add, ALU.mult))
            link(dve.tensor_reduce(rank_f[:], running.rearrange("p (k c) -> p c k", k=BUCKETS), AX, ALU.add))
            link(dve.tensor_scalar(rank_i[:, 0, :], rank_f[:], -1.0, None, ALU.add))
            link(dve.tensor_scalar(rank_i[:, 1, :], rank_i[:, 0, :], 7, None, ALU.logical_shift_right))
            link(dve.tensor_scalar(rank_i[:, 0, :], rank_i[:, 0, :], P - 1, None, ALU.bitwise_and))
            link(dve.scalar_tensor_tensor(nrow[:, :, ROW], rank_i[:, 0, :], float(TILES), rank_i[:, 1, :], ALU.mult, ALU.add))
            stage_rows(nrow, TILES, EC)

            for a in (1, 2):
                score_columns(a)
            link(dve.memset(near[:], 0.0))
            dve.wait_ge(bias_t_in, 16 * 3)
            link(dve.tensor_scalar(bias_t[:, 0:2, 0:D // P], bias_t[:, 0:2, 0:D // P], -1.0, None, ALU.add))

            dve.wait_ge(places_in, 16)
            link(dve.tensor_copy(idx_tab[:, :, 0], nload[:, :, NODE]))
            for k in range(3):
                link(dve.tensor_scalar(rank_f[:], nload[:, :, LEN], float(k), float(FAR), ALU.is_le, ALU.mult))
                link(dve.tensor_tensor(idx_tab[:, :, 1 + k], rank_f[:], nload[:, :, SRC + k], ALU.add))
                link(dve.tensor_scalar(mask_tab[:, :, 1 + k], nload[:, :, LEN], float(k), NONE, ALU.is_le, ALU.mult))
            link(dve.tensor_scalar(mask_tab[:, :, 0], nload[:, :, SELF], 0.0, NONE, ALU.is_equal, ALU.mult))
            link(dve.tensor_copy(len_tab[:, :, 1], nload[:, :, START]))
            dve.tensor_copy(len_tab[:, :, 0], nload[:, :, LEN]).then_inc(lens_ready, 1)
            dve.wait_ge(lens_ready, 1)
            link(dve.memset(more[:], 0.0))
            dve.sem_inc(extra_used, 1)
            dve.wait_ge(lens_turned, 1)
            dve.tensor_reduce(most[0:TILES, 0:1], tps[0:TILES, 0:P], AX, ALU.max).then_inc(most_ready, 1)
            dve.wait_ge(most_turned, 1)
            link(dve.memset(sched[:], 0))
            link(dve.memset(most[0:1, :], 0.0))
            for least, place in ((2, SEVERAL), (3, TRIPLE), (4, FURTHER)):
                link(dve.tensor_scalar(most[0:1, 0:TILES], tps[0:1, 512:512 + TILES], float(least), None, ALU.is_ge))
                link(dve.tensor_reduce(most[0:1, place:place + 1], most[0:1, 0:TILES], AX, ALU.add))
            link(dve.tensor_scalar(most[0:1, 0:TILES], tps[0:1, 512:512 + TILES], -2.0, 0.0, ALU.add, ALU.max))
            link(dve.tensor_copy(sched[0:1, 0:TILES], most[0:1, 0:TILES]))
            link(dve.tensor_scalar(sched[0:1, 0:TILES], sched[0:1, 0:TILES], 1, None, ALU.logical_shift_right))
            link(dve.tensor_copy(most[0:1, 0:TILES], sched[0:1, 0:TILES]))
            link(dve.tensor_tensor_scan(most[0:1, STEPS + 1:STEPS + 1 + TILES], one_row[0:1, 0:TILES], most[0:1, 0:TILES],
                                        0.0, ALU.mult, ALU.add))
            link(dve.tensor_copy(sched[0:1, STEPS:SEVERAL + 1], most[0:1, STEPS:SEVERAL + 1]))
            link(dve.tensor_scalar(most[0:1, SEVERAL_OF:SEVERAL_OF + 1], most[0:1, SEVERAL:SEVERAL + 1], 1.0, None, ALU.add))
            link(dve.tensor_copy(most[0:1, SEVERAL_OF + 1:SEVERAL_OF + 2], most[0:1, SEVERAL:SEVERAL + 1]))
            link(dve.tensor_copy(sched[0:1, SEVERAL_OF:SEVERAL_OF + 2], most[0:1, SEVERAL_OF:SEVERAL_OF + 2]))
            dve.tensor_scalar(sched[0:1, SEVERAL_OF:SEVERAL_OF + 2], sched[0:1, SEVERAL_OF:SEVERAL_OF + 2], 1, None,
                              ALU.logical_shift_right).then_inc(tables_ready, 1)
            dve.wait_ge(tables_ready, 1)

            score_columns(SPLIT[0])
            dve.sem_inc(early_used, 1)
            score_columns(SPLIT[1])

            rows_before = [0, 0]
            links_before = chained[0]
            for a in range(5):
                L = LAYERS[a]
                H = L.heads
                norm = AFTER[a].startswith("norm")
                base = a * TILES
                further = dve.value_load(sched[0:1, FURTHER:FURTHER + 1], min_val=0, max_val=TILES)
                several = dve.value_load(sched[0:1, SEVERAL:SEVERAL + 1], min_val=0, max_val=TILES)
                several_of = [dve.value_load(sched[0:1, SEVERAL_OF + i:SEVERAL_OF + i + 1], min_val=0, max_val=TILES) for i in range(2)]
                triple = dve.value_load(sched[0:1, TRIPLE:TRIPLE + 1], min_val=0, max_val=TILES)
                total = dve.value_load(sched[0:1, STEPS + TILES:STEPS + TILES + 1], min_val=0, max_val=EDGES)
                step_base = total * a
                per_tile = [0]
                late = 2 if norm else 1
                kept = expo if norm else acc[:, 0]
                keeps_before = sum(1 for M in LAYERS[:a] if M.residual)
                if norm:
                    dve.wait_ge(bias_in, 16 if a == 2 else 32)
                if a == 3:
                    for i in range(2):
                        dve.wait_ge(y_out[i], 16 * USES[i])

                def weighted(T, target, rows, weight):
                    if H == 1:
                        return [lambda: dve.scalar_tensor_tensor(target, rows, weight, target, ALU.mult, ALU.add)]
                    product = near[:, T.par, 1, 0:L.out]
                    return [lambda: dve.tensor_tensor(heads_of(product, L), heads_of(rows, L), over_dim(weight, L), ALU.mult),
                            lambda: dve.tensor_tensor(target, target, product, ALU.add)]

                def times(ap, n):
                    return ap.unsqueeze(1).to_broadcast([P, n, H])

                def total_of(T):
                    return (acc if norm else h)[:, T.par, 0:L.out]

                def own_er(T):
                    return near[:, T.par, 0, L.out + H:L.out + 2 * H]

                def linker(signal, start, here):
                    def link(ins):
                        ins.then_inc(signal, 1)
                        here[0] += 1
                        dve.wait_ge(signal, start + here[0])
                    return link

                def scores(T):
                    here = [0]
                    link = linker(schain, (T.t + base) * 5, here)
                    alone(dve)
                    with dve.If(several > T.t):
                        dve.wait_ge(gathered_more[T.par], (several_of[T.par] * a + T.use) * 32 + 32)
                        alone(dve)
                    dve.wait_ge(gathered[T.par], (T.use * 2 + (rows_before[T.par] + 2)) * 16)
                    rows = near[:, T.par]
                    e = e_s[:, :, 0:H]
                    link(dve.tensor_tensor(e, rows[:, :, L.out:L.out + H], times(own_er(T), 4), ALU.add))
                    link(dve.scalar_tensor_tensor(e, e, SLOPE, e, ALU.mult, ALU.max))
                    link(dve.tensor_tensor(e, e, mask_tab[:, bass.ds(T.t, 1), :].rearrange("p t k -> p (t k)").unsqueeze(2).to_broadcast([P, 4, H]), ALU.add))
                    link(dve.scalar_tensor_tensor(half[:, :, 0:H], e_s[:, 0:2, 0:H], FLOOR, e_s[:, 2:4, 0:H], ALU.max, ALU.max))
                    link(dve.tensor_tensor(m_s[:, T.par, 0:H], half[:, 0, 0:H], half[:, 1, 0:H], ALU.max))
                    assert here[0] == 5
                    dve.tensor_tensor(dif[:, T.par, :, 0:H], e, times(m_s[:, T.par, 0:H], 4), ALU.subtract).then_inc(dif_ready, 1)

                def sums(T, link):
                    total_ = total_of(T)
                    rows = near[:, T.par]
                    dve.wait_ge(exp_ready, T.t + base + 1)
                    p4 = p_s[:, T.par, :, 0:H]
                    link(dve.scalar_tensor_tensor(half[:, :, 0:H], p4[:, 0:2, :], L.eps / 2, p4[:, 2:4, :], ALU.add, ALU.add))
                    link(dve.tensor_tensor(den[:, 0, 0:H], half[:, 0, 0:H], half[:, 1, 0:H], ALU.add))
                    link(dve.reciprocal(rden[:, 0:H], den[:, 0, 0:H]))
                    link(dve.tensor_tensor(w_s[:, :, 0:H], p4, times(rden[:, 0:H], 4), ALU.mult))
                    if L.residual:
                        link(dve.tensor_scalar(w_s[:, 0, 0:H], w_s[:, 0, 0:H], 1.0, None, ALU.add))

                    if a == 4:
                        dve.wait_ge(summed, T.t + 1)
                    if norm and not (isinstance(T.t, int) and T.t + 2 * (a == 4) < 2):
                        dve.wait_ge(normed_ready, T.t + (TILES * (1 if a == 4 else 0) - 1))
                    if not norm and (a > 0 or not (isinstance(T.t, int) and T.t < 2)):
                        dve.wait_ge(turned, T.t + base - 1)
                    alone(dve)

                    def weigh_rows(n):
                        view = rows[:, 0:n, 0:L.out].rearrange("p k (h d) -> p k h d", h=H)
                        return dve.tensor_tensor(view, view, w_s[:, 0:n, 0:H].unsqueeze(3).to_broadcast([P, n, H, L.dim]), ALU.mult)

                    def sum_rows(n):
                        if H == 1:
                            two = dict(g=2)
                            start = zps[:, T.par, 0:2, 0:D // 2] if a == 4 else bias[:].rearrange("p (g n) -> p g n", **two)
                            todo = [lambda: dve.scalar_tensor_tensor(total_.rearrange("p (g n) -> p g n", **two), rows[:, 0, 0:L.out].rearrange("p (g n) -> p g n", **two),
                                                                     w_s[:, 0, 0:1], start, ALU.mult, ALU.add)]
                            todo += [lambda k=k: dve.scalar_tensor_tensor(total_, rows[:, k, 0:L.out], w_s[:, k, 0:1], total_, ALU.mult, ALU.add)
                                     for k in range(1, n)]
                        else:
                            todo = [lambda: weigh_rows(n)]
                            if n == 4:
                                todo += [lambda: dve.tensor_tensor(rows[:, 0:2, 0:L.out], rows[:, 0:2, 0:L.out], rows[:, 2:4, 0:L.out], ALU.add)]
                            todo += [lambda: dve.tensor_tensor(total_, rows[:, 0, 0:L.out], rows[:, 1, 0:L.out], ALU.add)]
                            if n == 3:
                                todo += [lambda: dve.tensor_tensor(total_, total_, rows[:, 2, 0:L.out], ALU.add)]
                        for k, make in enumerate(todo[:-1]):
                            make().then_inc(nchain, 1)
                            dve.wait_ge(nchain, (T.t + base) * 4 + (k + 1))
                        todo[-1]().then_inc(nchain, 5 - len(todo))

                    with dve.If(several > T.t):
                        with dve.If(triple > T.t):
                            if L.residual:
                                with dve.If(further > T.t):
                                    dve.tensor_copy(kept[:, 0:L.out], rows[:, 0, 0:L.out]).then_inc(fchain, 1)
                                    dve.wait_ge(fchain, further * keeps_before + T.t + 1)
                                    alone(dve)
                            sum_rows(4)
                            with dve.If(further > T.t):
                                dve.wait_ge(nchain, (T.t + base) * 4 + 4)
                                n = dve.value_load(sched[0:1, bass.ds(T.t, 1)], min_val=1, max_val=EDGES)
                                done = dve.value_load(sched[0:1, bass.ds(T.t + STEPS, 1)], min_val=0, max_val=EDGES)
                                dve.tensor_copy(xslot[:], slots[:, 2:4]).then_inc(slot_chain, 1)
                                dve.wait_ge(slot_chain, further * a + T.t + 1)
                                alone(dve)
                                with dve.Fori(0, n) as j:
                                    extra_step(T, done, j)
                        with dve.Else():
                            sum_rows(3)
                    with dve.Else():
                        sum_rows(2)
                    dve.wait_ge(nchain, (T.t + base) * 4 + 4)

                X_LINKS = [23, 23, 21, 20, 21]

                def extra_step(T, done, j):
                    here = [0]
                    total_, rows = total_of(T), more[:]
                    link = linker(xchain, total * sum(X_LINKS[:a]) + (done + j) * X_LINKS[a], here)
                    dve.wait_ge(extra_in, (step_base + done + j) * 32 + 32)
                    e = xe_s[:, :, 0:H]
                    m0, m1 = m_s[:, T.par, 0:H], xm_s[:, 0:H]
                    link(dve.tensor_scalar(xmask[:], xslot[:], len_tab[:, bass.ds(T.t, 1), 0:1].rearrange("p t k -> p (t k)"), NONE, ALU.is_ge, ALU.mult))
                    link(dve.tensor_scalar(xslot[:], xslot[:], 2.0, None, ALU.add))
                    link(dve.tensor_tensor(e, rows[:, :, L.out:L.out + H], times(own_er(T), 2), ALU.add))
                    link(dve.scalar_tensor_tensor(e, e, SLOPE, e, ALU.mult, ALU.max))
                    link(dve.tensor_tensor(e, e, xmask[:].unsqueeze(2).to_broadcast([P, 2, H]), ALU.add))
                    link(dve.tensor_tensor(m1, xe_s[:, 0, 0:H], m0, ALU.max))
                    link(dve.tensor_tensor(m1, xe_s[:, 1, 0:H], m1, ALU.max))
                    link(dve.tensor_tensor(xdif[:, 0:2, 0:H], e, times(m1, 2), ALU.subtract))
                    dve.tensor_tensor(xdif[:, 2, 0:H], m0, m1, ALU.subtract).then_inc(xdif_ready, 1)
                    dve.wait_ge(xexp_ready, step_base + done + j + 1)
                    link(dve.tensor_copy(m0, m1))
                    link(dve.tensor_tensor(den[:, 1, 0:H], den[:, 0, 0:H], xp_s[:, 2, 0:H], ALU.mult))
                    link(dve.tensor_tensor(rden[:, 0:H], xp_s[:, 0, 0:H], xp_s[:, 1, 0:H], ALU.add))
                    link(dve.tensor_tensor(den[:, 0, 0:H], den[:, 1, 0:H], rden[:, 0:H], ALU.add))
                    link(dve.reciprocal(rden[:, 0:H], den[:, 0, 0:H]))
                    link(dve.tensor_tensor(xw_s[:, 2, 0:H], den[:, 1, 0:H], rden[:, 0:H], ALU.mult))
                    link(dve.tensor_tensor(xw_s[:, 0:2, 0:H], xp_s[:, 0:2, 0:H], times(rden[:, 0:H], 2), ALU.mult))
                    if H == 1:
                        link(dve.tensor_scalar(total_, total_, xw_s[:, 2, 0:1], None, ALU.mult))
                    else:
                        link(dve.tensor_tensor(heads_of(total_, L), heads_of(total_, L), over_dim(xw_s[:, 2, 0:H], L), ALU.mult))
                    for k in range(2):
                        for make in weighted(T, total_, rows[:, k, 0:L.out], xw_s[:, k, 0:H]):
                            link(make())
                    if L.residual or H == 1:
                        link(dve.tensor_scalar(xw_s[:, 3, 0:H], xw_s[:, 2, 0:H], -1.0, 1.0, ALU.mult, ALU.add))
                    if L.residual:
                        for make in weighted(T, total_, kept[:, 0:L.out], xw_s[:, 3, 0:H]):
                            link(make())
                    if H == 1:
                        for make in weighted(T, total_, bias[:], xw_s[:, 3, 0:H]):
                            link(make())
                    if a == 4:
                        for make in weighted(T, total_, resid[:, T.par, :], xw_s[:, 3, 0:H]):
                            link(make())
                    dve.sem_inc(extra_used, 1)
                    assert here[0] == X_LINKS[a], (a, here)

                def settle(T, link):
                    v = total_of(T)
                    if a == 2:
                        dve.wait_ge(resid_in[T.par], T.use * 16 + 16)
                        link(dve.tensor_tensor(v, v, resid[:, T.par, :], ALU.add))
                    if norm:
                        for g in range(2):
                            link(dve.bn_stats(stats[:, g, :], v[:, g * (D // 2):(g + 1) * (D // 2)]))
                        alone(dve)
                        mv, guess = mean_var[:, T.par, :], rstd[:, T.par, 0:1]
                        link(dve.bn_aggr(mv, stats[:].rearrange("p g s -> p (g s)")))
                        link(dve.tensor_scalar(mv[:, 1:2], mv[:, 1:2], LN_EPS, None, ALU.add))
                        link(dve.tensor_scalar(guess, mv[:, 1:2].bitcast(I32), 1, None, ALU.logical_shift_right))
                        dve.tensor_scalar(guess, guess, -1.0, float(RSQRT_BITS), ALU.mult, ALU.add).then_inc(acc_ready, 1)
                    else:
                        dve.sem_inc(h_ready, 1)
                    dve.sem_inc(rows_used, 1)

                def finish(T):
                    if AFTER[a] == "elu":
                        dve.wait_ge(elu_ready, T.t + base + 1)
                        dve.scalar_tensor_tensor(hT[:, T.par, 0:D], hT[:, T.par, 0:D], -1.0, expo[:, 0:D], ALU.max, ALU.add).then_inc(hT_ready, 1)
                    elif a + 1 in SPLIT:
                        dve.wait_ge(hi_ready, T.t + base - 2 * TILES + 1)
                        dve.tensor_tensor(hT_lo[:, T.par, 0:L.out], hT_full[:, T.par, 0:L.out],
                                          hT_hi[:, T.par, 0:L.out].bitcast(F32), ALU.subtract).then_inc(hT_ready, 1)

                def tile(T):
                    here = [0]
                    link = linker(chain, T.t * per_tile[0] + links_before, here)
                    sums(T, link)
                    settle(T, link)
                    if not (isinstance(T.t, int) and T.t == TILES - 1):
                        scores(T.ahead())
                    if not (isinstance(T.t, int) and T.t < late):
                        finish(T.back(late))
                    per_tile[0] = here[0]

                scores(Tile(0, 0, 0))
                tile_loop(dve, tile, 4, 1)
                for n in range(late - 1, -1, -1):
                    finish(LAST.back(n))
                if a + 2 in SPLIT:
                    split_weights(a + 2)
                links_before += TILES * per_tile[0]
                for i in range(2):
                    rows_before[i] += 2 * USES[i]


def ring_uses(cols, j):
    return cols // RING + (1 if j < cols % RING else 0)


_WEIGHTS = ["L0_gnn_W0", "L0_gnn_W1", "L0_gnn_W2", "L1_gnn_W1", "L1_gnn_W2"]
_LEFTS = ["L0_gnn_al0", "L0_gnn_al1", "L0_gnn_al2", "L1_gnn_att_src1", "L1_gnn_att_src2"]
_RIGHTS = ["L0_gnn_ar0", "L0_gnn_ar1", "L0_gnn_ar2", "L1_gnn_att_dst1", "L1_gnn_att_dst2"]
_BIASES = ["L0_gnn_b0", "L0_gnn_b1", "L0_gnn_b2", "L1_gnn_b1", "L1_gnn_b2"]


def kernel(**inputs):
    import numpy as np
    import concourse.bacc as bacc
    from concourse.bass_utils import run_bass_kernel_spmd

    arrays, aps = {}, {}
    nc = bacc.Bacc("TRN2", target_bir_lowering=False, num_devices=1)

    def give(name, a):
        a = np.ascontiguousarray(a)
        arrays["in_" + name] = a
        aps[name] = nc.dram_tensor("in_" + name, a.shape, mybir.dt.from_np(a.dtype), kind="ExternalInput").ap()

    x = np.asarray(inputs["x"])
    x_rows = np.concatenate([x, np.zeros((ROWS - NODES, D), x.dtype)])
    give("x_rows", x_rows)
    give("x_tiles", x_rows.reshape(TILES, P, D // P, P).transpose(0, 3, 2, 1).reshape(TILES, P, D))
    dst, src = np.asarray(inputs["dst"]), np.asarray(inputs["src"])
    far = np.full(EPAD - EDGES + 1, FAR, dst.dtype)
    give("dst_ext", np.concatenate([np.full(1, -1, dst.dtype), dst, far]))
    give("src_ext", np.concatenate([src, np.zeros(EPAD - EDGES + 2, src.dtype)]))
    give("edge_no", np.arange(EPAD, dtype=np.int32).reshape(P, EC))
    node_rows = np.zeros((ROWS, ROW), np.int32)
    node_rows[:, NODE] = np.arange(ROWS)
    give("node_rows", node_rows)
    turned = [a for a in range(5) if not AFTER[a].startswith("norm")]
    for a in turned:
        give(f"turned_bias{a}", np.asarray(inputs[_BIASES[a]]).reshape(-1, P).T)
    give("ident", np.eye(P, dtype=np.float32))
    give("before", np.triu(np.ones((P, P), np.float32), 1))
    for name in _WEIGHTS:
        w = np.asarray(inputs[name])
        give(name, w.T if name.startswith("L1") else w)
    for name in _LEFTS + _RIGHTS + _BIASES:
        give(name, np.asarray(inputs[name]).reshape(1, -1))
    out = nc.dram_tensor("out_rows", (ROWS, D), F32, kind="ExternalOutput").ap()
    gat_program(nc, aps["x_tiles"], aps["x_rows"], aps["dst_ext"], aps["src_ext"], aps["edge_no"], aps["node_rows"],
                aps["ident"], aps["before"], [aps[n] for n in _WEIGHTS], [aps[n] for n in _LEFTS],
                [aps[n] for n in _RIGHTS], [aps[n] for n in _BIASES], [aps[f"turned_bias{a}"] for a in turned], out)
    r = run_bass_kernel_spmd(nc, [arrays], core_ids=[0])
    return r.results[0]["out_rows"][:NODES]
```
